# Optimizing a Trainium2 kernel written in Bass

```python
import numpy as np
import jax
import jax.numpy as jnp

def _softmax(x, axis=-1):
    return jax.nn.softmax(x, axis=axis)

def _gelu(x):
    return jax.nn.gelu(x, approximate=True)

def _silu(x):
    return jax.nn.silu(x)

def _sigmoid(x):
    return jax.nn.sigmoid(x)

def _layernorm(x, axis=-1, eps=1e-05):
    m = jnp.mean(x, axis=axis, keepdims=True)
    v = jnp.var(x, axis=axis, keepdims=True)
    return (x - m) / jnp.sqrt(v + eps)

def _scatter_add(tgt, idx, src, axis=0):
    return tgt.at[idx].add(src)

def _segment_sum(src, seg, n):
    return jax.ops.segment_sum(src, seg, n)
kernel_name = 'mk_adj_ffn_d1_adj_r2_57984c'

def setup_inputs(seed: int=0):
    np.random.seed(seed)
    _w = jnp.asarray

    def _rec_inputs():
        import jax
        import jax.numpy as jnp
        _gk = jax.random.key(seed)
        x = -0.0005207 + 1.001 * jax.random.normal(jax.random.fold_in(_gk, 1), (4096, 128), jnp.float32)
        _a = jax.random.bernoulli(jax.random.fold_in(_gk, 2), 0.00390625, (4096, 4096))
        _a = jnp.logical_or(_a, jnp.swapaxes(_a, -1, -2))
        _a = jnp.logical_or(_a, jnp.eye(4096, dtype=bool))
        _af = _a.astype(jnp.float32)
        _af = _af * jax.random.uniform(jax.random.fold_in(_gk, 3), (4096, 4096), jnp.float32, 0.05, 1)
        adj = _af
        return (x, adj)
    x, adj = _rec_inputs()

    def _L0_gnn_setup():
        import jax, jax.numpy as jnp
        import numpy as np
        N = 4096
        F_IN = 128
        F_OUT = 128
        key = jax.random.key(seed)
        k_x, k_adj, k_kernel, k_bias, k_beta = jax.random.split(key, 5)
        x = jax.random.normal(k_x, (N, F_IN), dtype=jnp.float32)
        adj = jax.random.uniform(k_adj, (N, N), dtype=jnp.float32)
        limit = float(np.sqrt(6.0 / (F_IN + F_OUT)))
        kernel = jax.random.uniform(k_kernel, (F_IN, F_OUT), dtype=jnp.float32, minval=-limit, maxval=limit)
        bias = 0.01 * jax.random.normal(k_bias, (F_OUT,), dtype=jnp.float32)
        beta = 0.01 * jax.random.normal(k_beta, (N,), dtype=jnp.float32)
        return {'x': x, 'adj': adj, 'kernel': kernel, 'bias': bias, 'beta': beta}
    _L0_gnn_all = _L0_gnn_setup()
    _L0_gnn_in = {k: v for k, v in _L0_gnn_all.items() if k in ('kernel', 'bias', 'beta')}
    del _L0_gnn_all

    def _L0_ffn_setup():
        import jax, jax.numpy as jnp
        import numpy as np
        D_IN, D_HID, D_OUT = (128, 256, 128)
        N_EXPERTS, TOP_K = (64, 2)
        B, S = (8, 2048)
        key = jax.random.key(seed)
        ks = jax.random.split(key, 8)
        scale_in = 1.0 / np.sqrt(D_IN)
        scale_hid = 1.0 / np.sqrt(D_HID)
        return {'x': jax.random.normal(ks[0], (B, S, D_IN), dtype=jnp.float32), 'Wr': jax.random.uniform(ks[1], (D_IN, N_EXPERTS), jnp.float32, -scale_in, scale_in), 'br': jax.random.uniform(ks[2], (N_EXPERTS,), jnp.float32, -scale_in, scale_in), 'W1': jax.random.uniform(ks[3], (N_EXPERTS, D_IN, D_HID), jnp.float32, -scale_in, scale_in), 'b1': jax.random.uniform(ks[4], (N_EXPERTS, D_HID), jnp.float32, -scale_in, scale_in), 'W2': jax.random.uniform(ks[5], (N_EXPERTS, D_HID, D_OUT), jnp.float32, -scale_hid, scale_hid), 'b2': jax.random.uniform(ks[6], (N_EXPERTS, D_OUT), jnp.float32, -scale_hid, scale_hid)}
    _L0_ffn_all = _L0_ffn_setup()
    _L0_ffn_in = {k: v for k, v in _L0_ffn_all.items() if k in ('Wr', 'br', 'W1', 'b1', 'W2', 'b2')}
    del _L0_ffn_all
    return {'x': x, 'adj': adj, 'L0_gnn_kernel': _L0_gnn_in['kernel'], 'L0_gnn_bias': _L0_gnn_in['bias'], 'L0_gnn_beta': _L0_gnn_in['beta'], 'L0_ffn_Wr': _L0_ffn_in['Wr'], 'L0_ffn_br': _L0_ffn_in['br'], 'L0_ffn_W1': _L0_ffn_in['W1'], 'L0_ffn_b1': _L0_ffn_in['b1'], 'L0_ffn_W2': _L0_ffn_in['W2'], 'L0_ffn_b2': _L0_ffn_in['b2']}

def reference(x, adj, L0_gnn_kernel, L0_gnn_bias, L0_gnn_beta, L0_ffn_Wr, L0_ffn_br, L0_ffn_W1, L0_ffn_b1, L0_ffn_W2, L0_ffn_b2):
    import jax
    import jax.numpy as jnp

    def _L0_gnn_ref(x, adj, kernel, bias, beta):
        import jax, jax.numpy as jnp
        import numpy as np
        N = 4096
        F_IN = 128
        F_OUT = 128
        scale = jnp.reciprocal(jnp.sum(adj, axis=1) + beta)
        agg = adj @ x + beta[:, None] * x
        return scale[:, None] * agg @ kernel + bias

    def _L0_ffn_ref(x, Wr, br, W1, b1, W2, b2):
        import jax, jax.numpy as jnp
        import numpy as np
        D_IN, D_HID, D_OUT = (128, 256, 128)
        N_EXPERTS, TOP_K = (64, 2)
        B, S = (8, 2048)
        Bx, Sx, D = x.shape
        xf = x.reshape(-1, D)
        T = xf.shape[0]
        E = Wr.shape[1]
        logits = xf @ Wr + br
        topk_logits, topk_idx = jax.lax.top_k(logits, TOP_K)
        gates = jax.nn.softmax(topk_logits, axis=1)
        combine = jnp.zeros((T, E), xf.dtype).at[jnp.arange(T)[:, None], topk_idx].add(gates)
        out = jnp.zeros((T, W2.shape[-1]), xf.dtype)
        for e in range(E):
            h = jax.nn.relu(xf @ W1[e] + b1[e])
            y = h @ W2[e] + b2[e]
            out = out + combine[:, e:e + 1] * y
        return out.reshape(Bx, Sx, -1)
    x = x + _L0_gnn_ref(_layernorm(x, axis=-1), adj, L0_gnn_kernel, L0_gnn_bias, L0_gnn_beta)
    x = x + _L0_ffn_ref(_layernorm(x, axis=-1)[None], L0_ffn_Wr, L0_ffn_br, L0_ffn_W1, L0_ffn_b1, L0_ffn_W2, L0_ffn_b2)[0]
    return x

_drawn_inputs = setup_inputs


def setup_inputs(seed=0):
    import zlib

    import numpy as np

    out = dict(_drawn_inputs(seed))
    spreads = {}
    factors = {'L0_gnn_bias': 2.908, 'L0_gnn_beta': 35.933, 'L0_ffn_b1': 3.96}
    for name, (base, spread) in spreads.items():
        noise = np.random.default_rng([zlib.crc32(name.encode()), seed]).standard_normal(out[name].shape)
        drawn = base * np.exp(spread * noise) if base else spread * noise
        out[name] = jnp.asarray(drawn.astype(out[name].dtype))
    for name, factor in factors.items():
        out[name] = (out[name] * factor).astype(out[name].dtype)
    return out
```

```python
from contextlib import ExitStack

import numpy as np

import concourse.bass as bass
from concourse import mybir

ALU = mybir.AluOpType
ACT = mybir.ActivationFunctionType
AX_X = mybir.AxisListType.X
F32 = mybir.dt.float32
BF16 = mybir.dt.bfloat16
I32 = mybir.dt.int32
U32 = mybir.dt.uint32

P = 128
N = 4096
D = 128
H = 256
E = 64
K = 2
EPS = 1e-5
HC = H // P
TILES = N // P
GT = 4
GN = GT * P
GROUPS = N // GN
CJ = 4
CHUNKS = TILES // CJ
ROW = D + 4
ANSWER = D
EXPERT_ROWS = N
SPARE = E * EXPERT_ROWS
NO_ANSWER = 1 << 20
SKIP = 1 << 21
WCOLS = H + HC * D + HC
QUAD = 4
SLOTS = 8
TILE_CAP = N * K // P + E
OCTETS = TILE_CAP // SLOTS
OUT_CH = 4


def lone_wait(eng, semaphore, value, passed):
    eng.wait_ge(semaphore, value)
    eng.sem_inc(passed, 1)


class Steps:

    def __init__(self, eng, sem):
        self.eng, self.sem, self.n, self.turn, self.per, self.start = eng, sem, 0, None, 0, 0

    def after(self, instruction, passed=None):
        instruction.then_inc(self.sem, 1)
        self.n += 1
        if passed is None:
            self.eng.wait_ge(self.sem, self.value())
        else:
            lone_wait(self.eng, self.sem, self.value(), passed)

    def value(self):
        if self.turn is None:
            return self.n
        return self.turn * self.per + self.n

    def enter(self, turn, per):
        self.turn, self.per, self.start = turn, per, self.n

    def leave(self, turns):
        assert self.n - self.start == self.per, (self.n - self.start, self.per)
        self.turn, self.n = None, self.start + self.per * turns


def program(nc, x, adj_t, gnn_w, gnn_b, beta, wr, br, w_pack, b2, out):
    rows = nc.dram_tensor("dispatched_rows", [SPARE + P, ROW], F32).ap()
    y_tok = nc.dram_tensor("expert_answers", [N * K, D], F32).ap()
    with ExitStack() as ctx:
        def sb(name, shape, dt=F32):
            return ctx.enter_context(nc.sbuf_tensor(name, shape, dt))

        def sem(name):
            return ctx.enter_context(nc.semaphore(name))

        bank = [ctx.enter_context(nc.psum_tensor(f"bank{i}", [P, 512], F32)) for i in range(8)]
        agg_ps = [bank[0], bank[1]]
        gnn_ps = bank[2][:].rearrange("p (t f) -> p t f", t=GT)
        turn_ps = bank[3]
        logit_ps = bank[4][:, 0:GT * E].rearrange("p (t e) -> p t e", t=GT)
        deg_ps = bank[4][:, GT * E:GT * E + GT]
        rank_ps = bank[5][:, 0:GT * E].rearrange("p (t e) -> p t e", t=GT)
        xt_ps = [bank[6], bank[7]]
        up_ps = [bank[0], bank[1]]
        down_ps = [bank[2], bank[3]]
        last_ps = bank[5]

        adj_sb = sb("adj_ring", [P, CHUNKS, CJ, GN])
        x_sb = sb("x_sb", [P, TILES, D])
        z_sb = sb("z_sb", [P, TILES, D])
        gnn_w_sb = sb("gnn_w_sb", [P, D])
        gnn_wd = sb("gnn_w_less_last_row", [P, D])
        gnn_b_sb = sb("gnn_b_sb", [P, D])
        wr_sb = sb("wr_sb", [P, E])
        br_sb = sb("br_sb", [P, E])
        b2_sb = sb("b2_sb", [E, D])
        beta_sb = sb("beta_sb", [P, TILES])
        ident = sb("ident", [P, P])
        last_row = sb("last_row", [P, P])
        before = sb("before", [P, P], BF16)
        ones_b = sb("ones_b", [P, P], BF16)
        ones_f = sb("ones_f", [P, P])
        iota_e = sb("iota_e", [P, E])
        iota_row = sb("iota_row", [P, P])
        iota_part = sb("iota_part", [P, 1])
        answer_tab = sb("answer_tab", [P, TILES, K])
        eps_sb = sb("eps_sb", [P, 1])
        pad_row = sb("pad_row", [P, ROW])
        stats = sb("stats", [P, GT, 6])
        mv = sb("mv", [P, GT, 2])
        std = sb("std", [P, GT])
        rstd = sb("rstd", [P, GT])
        zi = sb("zi", [P, GT, D])
        diag = sb("diag", [P, GT, P])
        agg_sb = sb("agg_sb", [P, GN])
        scale = sb("scale", [P, GT])
        x1 = sb("x1", [P, GT, D])
        payload = sb("payload", [P, GT, K, ROW])
        z1t = sb("z1t", [P, GN])
        logits = sb("logits", [P, GT, E])
        top = sb("top", [P, GT, 8])
        top_i = sb("top_i", [P, GT, 8], U32)
        chosen = sb("chosen", [P, GT, K])
        hot = sb("hot", [P, GT, K, E])
        mask = sb("mask", [P, GT, E], BF16)
        seen = sb("seen", [P, GT + 1, E], BF16)
        diff = sb("diff", [P, GT])
        ex = sb("ex", [P, GT])
        den = sb("den", [P, GT])
        gates = sb("gates", [P, TILES, K])
        work = sb("work", [P, GT, K, E])
        rank = sb("rank", [P, GT * K])
        slot = sb("slot", [P, GT * K], I32)
        comb = sb("comb", [P, GT, E])
        combt = sb("combt", [E, GN])
        cnt = sb("cnt", [P, E])
        cnt_i = sb("cnt_i", [P, E], I32)
        tiles_i = sb("tiles_i", [P, E], I32)
        tiles_f = sb("tiles_f", [P, E])
        upto = sb("upto", [P, E])
        past = sb("past", [P, E])
        lw = sb("lw", [P, E])
        lc = sb("lc", [P, 16])
        lst = sb("lst", [P, 4])
        q_i = sb("q_i", [P, 2], I32)
        ov_diag = sb("ov_diag", [P, P])
        skip_tab = sb("skip_tab", [P, P])
        table = sb("table", [4, P], I32)
        w_sb = sb("w_sb", [P, SLOTS, WCOLS])
        xin = sb("xin", [P, SLOTS, ROW])
        xt_sb = sb("xt_sb", [P, 2, P])
        h_sb = sb("h_sb", [P, 2, HC, P])
        y_sb = sb("y_sb", [P, SLOTS, D])
        ans = sb("ans", [P, SLOTS], I32)
        y_in = sb("y_in", [P, TILES, K, D])
        o_sb = sb("o_sb", [P, TILES, D])

        x_in = sem("x_in")
        params_in = sem("params_in")
        adj_in = [sem(f"adj_in{k}") for k in range(CHUNKS)]
        prefilled = sem("prefilled")
        consts = sem("consts")
        passed = sem("passed")
        pool_own = sem("pool_own")
        dve_own = sem("dve_own")
        act_own = sem("act_own")
        var0 = sem("var0")
        std0 = sem("std0")
        z_ready = sem("z_ready")
        bias_added = sem("bias_added")
        wrow_done = sem("wrow_done")
        wd_ready = sem("wd_ready")
        chunk_used = sem("chunk_used")
        own_ready = sem("own_ready")
        agg_done = sem("agg_done")
        agg_copied = sem("agg_copied")
        gnn_done = sem("gnn_done")
        var1 = sem("var1")
        std1 = sem("std1")
        z1_ready = sem("z1_ready")
        z1_turned = sem("z1_turned")
        z1t_ready = sem("z1t_ready")
        logits_done = sem("logits_done")
        mask_ready = sem("mask_ready")
        rank_done = sem("rank_done")
        diff_ready = sem("diff_ready")
        ex_ready = sem("ex_ready")
        slots_ready = sem("slots_ready")
        payload_free = sem("payload_free")
        scattered = sem("scattered")
        comb_ready = sem("comb_ready")
        comb_turned = sem("comb_turned")
        combt_ready = sem("combt_ready")
        b2_done = sem("b2_done")
        base_ready = sem("base_ready")
        total_ready = sem("total_ready")
        total_done = sem("total_done")
        list_ready = sem("list_ready")
        list_turned = sem("list_turned")
        table_ready = sem("table_ready")
        tile_in = [sem(f"tile_in{s}") for s in range(SLOTS)]
        x_turned = sem("x_turned")
        xt_ready = sem("xt_ready")
        up_done = sem("up_done")
        h_ready = sem("h_ready")
        down_done = sem("down_done")
        y_ready = sem("y_ready")
        y_out = [sem(f"y_out{s}") for s in range(SLOTS)]
        y_back = [sem(f"y_back{c}") for c in range(4)]
        o_ready = sem("o_ready")
        stored = sem("stored")

        BUFS = 2

        def quads_in_use(eng):
            return eng.value_load(table[2:3, 0:1], min_val=TILE_CAP // 2 // QUAD, max_val=TILE_CAP // QUAD)

        block = ctx.enter_context(nc.Block())

        @block.sync
        def _(sp):
            sp.dma_start(x_sb[:], x.rearrange("(t p) f -> p t f", p=P)).then_inc(x_in, 16)

            def load_chunk(g, k):
                sp.dma_start(adj_sb[:, k], adj_t[g, k] if isinstance(g, int) else adj_t[bass.ds(g, 1), k].rearrange("a p u n -> (a p) u n")).then_inc(adj_in[k], 16)

            for k in range(CHUNKS):
                load_chunk(0, k)
                if k == 0:
                    sp.dma_start(gnn_w_sb[:], gnn_w).then_inc(params_in, 16)
                    sp.dma_start(beta_sb[:], beta).then_inc(params_in, 16)
                    sp.dma_start(gnn_b_sb[:], gnn_b.partition_broadcast(P)).then_inc(params_in, 16)
                    sp.dma_start(wr_sb[:], wr).then_inc(params_in, 16)
                    sp.dma_start(br_sb[:], br.partition_broadcast(P)).then_inc(params_in, 16)
                    sp.dma_start(b2_sb[:], b2).then_inc(params_in, 16)
            sp.wait_ge(consts, 1)
            sp.dma_start(rows[0:SPARE, :].rearrange("(e s) c -> s e c", e=E)[0:P],
                         pad_row[:, None, :].to_broadcast([P, E, ROW])).then_inc(prefilled, 16)
            sp.dma_start(rows[SPARE:SPARE + P, :], pad_row[:]).then_inc(prefilled, 16)
            with sp.Fori(1, GROUPS) as g:
                for k in range(CHUNKS):
                    sp.wait_ge(chunk_used, g * CHUNKS + (k + 1 - CHUNKS))
                    load_chunk(g, k)

            def load_quad(quad, slot0, turn):
                experts = [sp.value_load(table[0:1, bass.ds(quad * QUAD + s, 1)], min_val=0, max_val=E - 1)
                           for s in range(QUAD)]
                starts = [sp.value_load(table[1:2, bass.ds(quad * QUAD + s, 1)], min_val=0, max_val=SPARE)
                          for s in range(QUAD)]
                for s in range(QUAD):
                    if turn is not None:
                        sp.wait_ge(y_out[slot0 + s], turn * 16 + 16)
                    sp.dma_start(w_sb[:, slot0 + s], w_pack[bass.ds(experts[s], 1)].rearrange("a p c -> (a p) c")).then_inc(tile_in[slot0 + s], 16)
                    if turn is None and s == 0:
                        sp.wait_ge(scattered, 16 * TILES * K)
                    sp.dma_start(xin[:, slot0 + s], rows[bass.ds(starts[s], P), :]).then_inc(tile_in[slot0 + s], 16)

            sp.wait_ge(table_ready, 1)
            quads = quads_in_use(sp)
            load_quad(0, 0, None)
            load_quad(1, QUAD, None)
            with sp.Fori(0, OCTETS - 1) as turn:
                for half in range(2):
                    with sp.If(turn * 2 + 2 + half < quads):
                        load_quad(turn * 2 + (2 + half), half * QUAD, turn)
            for s in range(SLOTS):
                sp.wait_ge(y_out[s], ((quads + (1 if s < QUAD else 0)) // 2) * 16)
            answers = y_tok.rearrange("(t p k) f -> p t k f", p=P, k=K)
            per = TILES // 4
            for c in range(4):
                sp.dma_start(y_in[:, c * per:(c + 1) * per], answers[:, c * per:(c + 1) * per]).then_inc(y_back[c], 16)
            for c in range(4):
                sp.wait_ge(o_ready, c + 1)
                sp.dma_start(out.rearrange("(t p) f -> p t f", p=P)[:, c * per:(c + 1) * per],
                             o_sb[:, c * per:(c + 1) * per]).then_inc(stored, 16)
            sp.wait_ge(stored, 64)

        @block.gpsimd
        def _(pool):
            own = Steps(pool, pool_own)
            pool.memset(pad_row[:], 0.0)
            pool.memset(ident[:], 0.0)
            pool.memset(last_row[:], 0.0)
            pool.memset(before[:], 0.0)
            pool.memset(ones_b[:], 1.0)
            pool.memset(ones_f[:], 1.0)
            pool.memset(seen[:], 0.0)
            pool.memset(eps_sb[:], EPS)
            own.after(pool.memset(payload[:], 0.0))
            pool.memset(pad_row[:, ANSWER:ANSWER + 1], float(NO_ANSWER))
            pool.affine_select(out=ident[:], in_=ident[:], compare_op=ALU.not_equal, fill=1.0, base=0,
                               pattern=[[-1, P]], channel_multiplier=1)
            pool.affine_select(out=last_row[:], in_=last_row[:], compare_op=ALU.not_equal, fill=1.0, base=1 - P,
                               pattern=[[0, P]], channel_multiplier=1)
            pool.affine_select(out=before[:], in_=before[:], compare_op=ALU.is_ge, fill=1.0, base=0,
                               pattern=[[-1, P]], channel_multiplier=1)
            pool.iota(iota_e[:], [[1, E]], base=0, channel_multiplier=0, allow_small_or_imprecise_dtypes=True)
            pool.iota(iota_row[:], [[1, P]], base=0, channel_multiplier=0, allow_small_or_imprecise_dtypes=True)
            pool.iota(iota_part[:], [[0, 1]], base=0, channel_multiplier=1, allow_small_or_imprecise_dtypes=True)
            pool.iota(answer_tab[:], [[P * K, TILES], [1, K]], base=0, channel_multiplier=K,
                      allow_small_or_imprecise_dtypes=True)
            own.after(pool.memset(z_sb[:, :, D - 1:D], 1.0))
            pool.sem_inc(consts, 1)
            pool.sem_inc(payload_free, 1)
            pool.wait_ge(params_in, 16 * 6)
            own.enter(None, 0)
            with pool.Fori(0, GROUPS) as c:
                lone_wait(pool, z_ready, c * GT + GT, passed)
                xs = x_sb[:, bass.ds(c * GT, GT), :]
                pool.tensor_tensor(xs, xs, gnn_b_sb[:, None, :].to_broadcast([P, GT, D]), ALU.add).then_inc(bias_added, 1)

            with pool.Fori(0, GROUPS) as g:
                lone_wait(pool, agg_done, g + 1, passed)
                pool.tensor_copy(zi[:], z_sb[:, bass.ds(g * GT, GT), :])
                pool.tensor_tensor(diag[:], ident[:, None, :].to_broadcast([P, GT, P]),
                                   beta_sb[:, bass.ds(g * GT, GT)].to_broadcast([P, GT, P]), ALU.mult).then_inc(own_ready, 1)
                lone_wait(pool, z1_ready, g + 1, passed)
                pool.tensor_copy(payload[:, :, 1, 0:D], payload[:, :, 0, 0:D]).then_inc(pool_own, 1)
                pool.tensor_copy(payload[:, :, :, ANSWER], answer_tab[:, bass.ds(g * GT, GT), :]).then_inc(pool_own, 1)
                lone_wait(pool, pool_own, g * 2 + (own.n + 2), passed)
                pool.wait_ge(prefilled, 32)
                lone_wait(pool, slots_ready, g + 1, passed)
                for t in range(GT):
                    for k in range(K):
                        i = t * K + k
                        pool.indirect_dma_start(rows, bass.IndirectOffsetOnAxis(ap=slot[:, i:i + 1], axis=0),
                                                payload[:, t, k, :], None).then_inc(scattered, 16)
                pool.wait_ge(scattered, g * (GT * K * 16) + GT * K * 16)
                pool.sem_inc(payload_free, 1)

            pool.wait_ge(table_ready, 1)
            quads = quads_in_use(pool)
            with pool.Fori(0, OCTETS) as turn:
                for half in range(2):
                    with pool.If(turn * 2 + half < quads):
                        for s in range(half * QUAD, half * QUAD + QUAD):
                            lone_wait(pool, y_ready, turn * SLOTS + (s + 1 + BUFS), passed)
                            pool.indirect_dma_start(y_tok, bass.IndirectOffsetOnAxis(ap=ans[:, s:s + 1], axis=0),
                                                    y_sb[:, s, :], None, bounds_check=N * K - 1,
                                                    oob_is_err=False).then_inc(y_out[s], 16)

        @block.scalar
        def _(act):
            act.wait_ge(consts, 1)
            with act.Fori(0, GROUPS) as c:
                act.wait_ge(var0, c + 1)
                nc.scalar.activation(std[:], mv[:, :, 1], ACT.Sqrt, bias=eps_sb[:]).then_inc(std0, 1)
            with act.Fori(0, GROUPS // 2) as pair:
                for b in range(2):
                    g1 = pair * 2 + (b + 1)
                    act.wait_ge(agg_done, g1 + 1)
                    nc.scalar.copy(agg_sb[:], agg_ps[b][:]).then_inc(agg_copied, 1)
                    act.wait_ge(var1, g1)
                    nc.scalar.activation(std[:], mv[:, :, 1], ACT.Sqrt, bias=eps_sb[:]).then_inc(std1, 1)
                    act.wait_ge(z1_turned, g1)
                    nc.scalar.copy(z1t[:], turn_ps[:]).then_inc(z1t_ready, 1)
                    act.wait_ge(diff_ready, g1)
                    nc.scalar.activation(ex[:], diff[:], ACT.Exp).then_inc(ex_ready, 1)
                    act.wait_ge(comb_turned, g1)
                    nc.scalar.copy(combt[:], turn_ps[0:E, :]).then_inc(combt_ready, 1)
            act.sem_inc(h_ready, BUFS)
            act.wait_ge(table_ready, 1)
            quads = quads_in_use(act)
            with act.Fori(0, OCTETS) as turn:
                for half in range(2):
                    with act.If(turn * 2 + half < quads):
                        for s in range(half * QUAD, half * QUAD + QUAD):
                            act.wait_ge(up_done, turn * SLOTS + (s + 1 + BUFS))
                            act.wait_ge(down_done, turn * SLOTS + (s + 1))
                            for c in range(HC):
                                last = nc.scalar.activation(h_sb[:, s % 2, c, :], up_ps[s % 2][:, c * P:(c + 1) * P],
                                                            ACT.Relu, bias=w_sb[:, s, H + HC * D + c:H + HC * D + c + 1])
                            last.then_inc(h_ready, 1)

        @block.vector
        def _(dve):
            own = Steps(dve, dve_own)
            v = nc.vector
            dve.wait_ge(consts, 1)
            dve.wait_ge(x_in, 16)
            with dve.Fori(0, GROUPS) as c:
                own.enter(c, 3)
                for t in range(GT):
                    last = v.bn_stats(stats[:, t, :], x_sb[:, bass.ds(c * GT + t, 1), :].rearrange("p a f -> p (a f)"))
                own.after(last, passed)
                for t in range(GT):
                    last = v.bn_aggr(mv[:, t, :], stats[:, t, :])
                last.then_inc(var0, 1)
                dve.wait_ge(std0, c + 1)
                own.after(v.reciprocal(rstd[:], std[:]))
                for t in range(GT):
                    xs = x_sb[:, bass.ds(c * GT + t, 1), 0:D - 1].rearrange("p a f -> p (a f)")
                    zs = z_sb[:, bass.ds(c * GT + t, 1), 0:D - 1].rearrange("p a f -> p (a f)")
                    v.tensor_scalar(zs, xs, mv[:, t, 0:1], rstd[:, t:t + 1], ALU.subtract, ALU.mult).then_inc(z_ready, 1)
                dve.wait_ge(z_ready, c * GT + GT)
                own.after(v.tensor_copy(std[:, 0:1], std[:, 0:1]))
                own.leave(GROUPS)
            dve.wait_ge(wrow_done, 1)
            v.tensor_tensor(gnn_wd[:], gnn_w_sb[:], bank[6][:, 0:D], ALU.subtract).then_inc(wd_ready, 1)
            dve.sem_inc(base_ready, 1)

            with dve.Fori(0, GROUPS) as g:
                own.enter(g, 22)
                dve.wait_ge(bias_added, g + 1)
                dve.wait_ge(gnn_done, g + 1)
                own.after(v.reciprocal(scale[:], deg_ps))
                own.after(v.tensor_tensor(x1[:], gnn_ps, scale[:].to_broadcast([P, GT, D]), ALU.mult))
                own.after(v.tensor_tensor(x1[:], x1[:], x_sb[:, bass.ds(g * GT, GT), :], ALU.add))
                for t in range(GT):
                    last = v.bn_stats(stats[:, t, :], x1[:, t, :])
                own.after(last, passed)
                for t in range(GT):
                    last = v.bn_aggr(mv[:, t, :], stats[:, t, :])
                last.then_inc(var1, 1)
                dve.wait_ge(std1, g + 1)
                own.after(v.reciprocal(rstd[:], std[:]))
                dve.wait_ge(payload_free, g + 1)
                for t in range(GT):
                    last = v.tensor_scalar(payload[:, t, 0, 0:D], x1[:, t, :], mv[:, t, 0:1], rstd[:, t:t + 1],
                                           ALU.subtract, ALU.mult)
                last.then_inc(z1_ready, 1)
                dve.wait_ge(logits_done, g + 1)
                own.after(v.tensor_tensor(logits[:], logit_ps, br_sb[:, None, :].to_broadcast([P, GT, E]), ALU.add), passed)
                for t in range(GT):
                    last = v.max(top[:, t, :], logits[:, t, :])
                own.after(last, passed)
                for t in range(GT):
                    last = v.max_index(top_i[:, t, :], top[:, t, :], logits[:, t, :])
                own.after(last)
                v.tensor_tensor(diff[:], top[:, :, 1], top[:, :, 0], ALU.subtract).then_inc(diff_ready, 1)
                own.after(v.tensor_copy(chosen[:], top_i[:, :, 0:K]))
                own.after(v.tensor_tensor(hot[:].rearrange("p t k e -> p (t k) e"),
                                          iota_e[:, None, :].to_broadcast([P, GT * K, E]),
                                          chosen[:].rearrange("p t k -> p (t k)").to_broadcast([P, GT * K, E]), ALU.is_equal))
                v.tensor_copy(seen[:, 0, :], seen[:, GT, :]).then_inc(dve_own, 1)
                own.n += 1
                own.after(v.tensor_tensor(mask[:], hot[:, :, 0, :], hot[:, :, 1, :], ALU.add))
                for t in range(GT):
                    own.after(v.tensor_tensor(seen[:, t + 1, :], seen[:, t, :], mask[:, t, :], ALU.add))
                dve.sem_inc(mask_ready, 1)
                dve.wait_ge(ex_ready, g + 1)
                own.after(v.tensor_scalar(den[:], ex[:], 1.0, None, ALU.add))
                gs = gates[:, bass.ds(g * GT, GT), :]
                own.after(v.reciprocal(den[:], den[:]))
                v.tensor_copy(gs[:, :, 0], den[:])
                own.after(v.tensor_tensor(gs[:, :, 1], ex[:], den[:], ALU.mult))
                dve.wait_ge(rank_done, g + 1)
                for k in range(K):
                    last = v.tensor_tensor(work[:, :, k, :], hot[:, :, k, :], rank_ps, ALU.mult)
                own.after(last)
                own.after(v.tensor_reduce(rank[:], work[:].rearrange("p t k e -> p (t k) e"), AX_X, ALU.add))
                v.scalar_tensor_tensor(out=slot[:], in0=chosen[:].rearrange("p t k -> p (t k)"), scalar=float(EXPERT_ROWS),
                                       in1=rank[:], op0=ALU.mult, op1=ALU.add).then_inc(slots_ready, 1)
                own.after(v.tensor_tensor(work[:].rearrange("p t k e -> p (t k) e"), hot[:].rearrange("p t k e -> p (t k) e"),
                                          gs.rearrange("p t k -> p (t k)").to_broadcast([P, GT * K, E]), ALU.mult))
                v.tensor_tensor(comb[:], work[:, :, 0, :], work[:, :, 1, :], ALU.add).then_inc(comb_ready, 1)
                dve.wait_ge(b2_done, g + 1)
                v.tensor_tensor(x_sb[:, bass.ds(g * GT, GT), :], gnn_ps, x1[:], ALU.add).then_inc(base_ready, 1)
                own.leave(GROUPS)

            dve.wait_ge(total_done, 1)
            own.after(v.tensor_copy(cnt[:], last_ps[:, 0:E]))
            own.after(v.tensor_scalar(cnt_i[:], cnt[:], float(P - 1), None, ALU.add))
            own.after(v.tensor_scalar(tiles_i[:], cnt_i[:], 7, None, ALU.logical_shift_right))
            own.after(v.tensor_copy(tiles_f[:], tiles_i[:]))
            own.after(v.tensor_tensor_scan(upto[:], tiles_f[:], ones_f[:, 0:E], 0.0, ALU.add, ALU.mult))
            used = upto[:, E - 1:E]
            own.after(v.tensor_scalar(past[:], upto[:], iota_part[:], None, ALU.is_le))
            own.after(v.tensor_reduce(lc[:, 0:1], past[:], AX_X, ALU.add))
            own.after(v.tensor_tensor(lw[:], past[:], upto[:], ALU.mult))
            own.after(v.tensor_reduce(lc[:, 1:2], lw[:], AX_X, ALU.max))
            own.after(v.tensor_scalar(past[:], iota_e[:], lc[:, 0:1], None, ALU.is_equal))
            own.after(v.tensor_tensor(lw[:], past[:], cnt[:], ALU.mult))
            own.after(v.tensor_reduce(lc[:, 2:3], lw[:], AX_X, ALU.add))
            own.after(v.tensor_tensor(lc[:, 3:4], iota_part[:], lc[:, 1:2], ALU.subtract))
            own.after(v.tensor_scalar(lc[:, 3:4], lc[:, 3:4], float(P), None, ALU.mult))
            own.after(v.tensor_scalar(lc[:, 4:5], lc[:, 2:3], float(-P), 0.0, ALU.add, ALU.max))
            own.after(v.tensor_tensor(lc[:, 5:6], lc[:, 3:4], lc[:, 4:5], ALU.min))
            own.after(v.tensor_tensor(lc[:, 6:7], lc[:, 3:4], lc[:, 5:6], ALU.subtract))
            own.after(v.tensor_tensor(lc[:, 7:8], iota_part[:], used, ALU.is_lt))
            own.after(v.scalar_tensor_tensor(out=lc[:, 8:9], in0=lc[:, 0:1], scalar=float(EXPERT_ROWS), in1=lc[:, 5:6],
                                             op0=ALU.mult, op1=ALU.add))
            own.after(v.tensor_scalar(lc[:, 9:10], lc[:, 8:9], float(-SPARE), lc[:, 7:8], ALU.add, ALU.mult))
            v.tensor_scalar(lst[:, 1:2], lc[:, 9:10], float(SPARE), None, ALU.add)
            v.tensor_tensor(lst[:, 0:1], lc[:, 0:1], lc[:, 7:8], ALU.mult)
            v.tensor_tensor(lc[:, 10:11], lc[:, 6:7], lc[:, 7:8], ALU.mult)
            own.after(v.tensor_scalar(q_i[:, 0:1], used, float(QUAD - 1), None, ALU.add))
            own.after(v.tensor_scalar(q_i[:, 1:2], q_i[:, 0:1], 2, None, ALU.logical_shift_right))
            v.tensor_copy(lst[:, 2:3], q_i[:, 1:2])
            v.tensor_copy(lst[:, 3:4], iota_part[:])
            own.after(v.tensor_scalar(ov_diag[:], ident[:], lc[:, 10:11], None, ALU.mult))
            dve.sem_inc(list_ready, 1)
            dve.wait_ge(list_turned, 1)
            own.after(v.tensor_copy(table[:], bank[6][0:4, 0:P]))
            own.after(v.tensor_scalar(skip_tab[:], bank[6][:, P:2 * P], iota_part[:], float(SKIP), ALU.is_gt, ALU.mult))
            dve.sem_inc(table_ready, 1)
            dve.sem_inc(xt_ready, BUFS)
            dve.sem_inc(y_ready, BUFS)

            quads = quads_in_use(dve)

            def copy_xt(turn, s):
                dve.wait_ge(x_turned, turn * SLOTS + (s + 1 + BUFS))
                dve.wait_ge(up_done, turn * SLOTS + (s + 1))
                v.tensor_copy(xt_sb[:, s % 2, :], xt_ps[s % 2][:, 0:P]).then_inc(xt_ready, 1)

            def copy_y(turn, s):
                v.tensor_tensor(ans[:, s:s + 1], xin[:, s, ANSWER:ANSWER + 1],
                                skip_tab[:, bass.ds(turn * SLOTS + s, 1)], ALU.add)
                dve.wait_ge(down_done, turn * SLOTS + (s + 1 + BUFS))
                v.tensor_copy(y_sb[:, s, :], down_ps[s % 2][:, 0:D]).then_inc(y_ready, 1)

            with dve.Fori(0, OCTETS) as turn:
                for half in range(2):
                    o = half * QUAD
                    with dve.If(turn * 2 + half < quads):
                        copy_xt(turn, o)
                        copy_xt(turn, o + 1)
                        copy_xt(turn, o + 2)
                        copy_y(turn, o)
                        copy_xt(turn, o + 3)
                        copy_y(turn, o + 1)
                        copy_y(turn, o + 2)
                        copy_y(turn, o + 3)

            per = TILES // 4
            for c in range(4):
                dve.wait_ge(y_back[c], 16)
                for t in range(c * per, (c + 1) * per):
                    v.scalar_tensor_tensor(out=o_sb[:, t, :], in0=y_in[:, t, 0, :], scalar=gates[:, t, 0:1],
                                           in1=x_sb[:, t, :], op0=ALU.mult, op1=ALU.add).then_inc(dve_own, 1)
                    own.n += 1
                for t in range(c * per, (c + 1) * per):
                    dve.wait_ge(dve_own, own.n - per + 1 + t - c * per)
                    last = v.scalar_tensor_tensor(out=o_sb[:, t, :], in0=y_in[:, t, 1, :], scalar=gates[:, t, 1:2],
                                                  in1=o_sb[:, t, :], op0=ALU.mult, op1=ALU.add)
                last.then_inc(o_ready, 1)

        @block.tensor
        def _(pe):
            mm = nc.tensor.matmul
            pe.wait_ge(consts, 1)
            pe.wait_ge(params_in, 16 * 6)
            pe.sem_inc(agg_done, 1)
            mm(bank[6][:, 0:D], last_row[:], gnn_w_sb[:], start=True, stop=True).then_inc(wrow_done, 1)

            def gnn(g):
                pe.wait_ge(wd_ready, 1)
                pe.wait_ge(base_ready, g + 1)
                pe.wait_ge(agg_copied, g + 1)
                for t in range(GT):
                    mm(gnn_ps[:, t, :], agg_sb[:, t * P:(t + 1) * P], gnn_wd[:], start=True, stop=True)
                for t in range(GT):
                    last = mm(deg_ps[:, t:t + 1], agg_sb[:, t * P:(t + 1) * P], last_row[:, 0:1], start=True, stop=True)
                last.then_inc(gnn_done, 1)

            def turn_z1(g):
                pe.wait_ge(z1_ready, g + 1)
                for t in range(GT):
                    last = nc.tensor.transpose(turn_ps[:, t * P:(t + 1) * P], payload[:, t, 0, 0:D], ident[:])
                last.then_inc(z1_turned, 1)

            def router(g):
                pe.wait_ge(z1t_ready, g + 1)
                for t in range(GT):
                    last = mm(logit_ps[:, t, :], z1t[:, t * P:(t + 1) * P], wr_sb[:], start=True, stop=True)
                last.then_inc(logits_done, 1)

            def ranks(g):
                pe.wait_ge(mask_ready, g + 1)
                mm(rank_ps, before[:], mask[:], start=True, stop=False)
                mm(rank_ps, ones_b[:], seen[:, 0:GT, :], start=False, stop=True).then_inc(rank_done, 1)

            def turn_comb(g):
                lone_wait(pe, comb_ready, g + 1, passed)
                for t in range(GT):
                    last = nc.tensor.transpose(turn_ps[0:E, t * P:(t + 1) * P], comb[:, t, :], ident[:])
                last.then_inc(comb_turned, 1)

            def bias2(g):
                pe.wait_ge(combt_ready, g + 1)
                for t in range(GT):
                    last = mm(gnn_ps[:, t, :], combt[:, t * P:(t + 1) * P], b2_sb[:], start=True, stop=True)
                last.then_inc(b2_done, 1)

            later = {2: gnn, 11: turn_z1, 14: router, 20: ranks, 26: turn_comb, 29: bias2}

            def aggregate(g, b, prev):
                for j in range(TILES):
                    if j % CJ == 0:
                        pe.wait_ge(adj_in[j // CJ], g * 16 + 16)
                    if prev is None:
                        pe.wait_ge(z_ready, j + 1)
                    elif j in later:
                        later[j](prev)
                    last = mm(agg_ps[b][:], z_sb[:, j, :], adj_sb[:, j // CJ, j % CJ, :], start=(j == 0), stop=False)
                    if j % CJ == CJ - 1:
                        last.then_inc(chunk_used, 1)
                pe.wait_ge(own_ready, g + 1)
                for t in range(GT):
                    last = mm(agg_ps[b][:, t * P:(t + 1) * P], zi[:, t, :], diag[:, t, :], start=False, stop=(t == GT - 1))
                last.then_inc(agg_done, 1)

            aggregate(0, 0, None)
            with pe.Fori(0, GROUPS // 2 - 1) as i:
                aggregate(i * 2 + 1, 1, i * 2)
                aggregate(i * 2 + 2, 0, i * 2 + 1)
            aggregate(GROUPS - 1, 1, GROUPS - 2)
            for step in later.values():
                step(GROUPS - 1)
                if step is ranks:
                    pe.wait_ge(slots_ready, GROUPS)
                    mm(last_ps[:, 0:E], ones_b[:], seen[:, GT, :], start=True, stop=True).then_inc(total_done, 1)
            pe.wait_ge(list_ready, 1)
            nc.tensor.transpose(bank[6][0:4, 0:P], lst[:], ident[:])
            mm(bank[6][:, P:2 * P], ones_f[:], ov_diag[:], start=True, stop=True).then_inc(list_turned, 1)

            pe.wait_ge(table_ready, 1)
            pe.wait_ge(base_ready, GROUPS + 1)
            pe.sem_inc(x_turned, BUFS)
            pe.sem_inc(up_done, BUFS)
            pe.sem_inc(down_done, BUFS)
            quads = quads_in_use(pe)

            def turn_x(turn, s):
                pe.wait_ge(tile_in[s], turn * 32 + 32)
                pe.wait_ge(xt_ready, turn * SLOTS + (s + 1))
                nc.tensor.transpose(xt_ps[s % 2][:, 0:P], xin[:, s, 0:D], ident[:]).then_inc(x_turned, 1)

            def up(turn, s):
                pe.wait_ge(xt_ready, turn * SLOTS + (s + 1 + BUFS))
                pe.wait_ge(h_ready, turn * SLOTS + (s + 1))
                for c in range(HC):
                    last = mm(up_ps[s % 2][:, c * P:(c + 1) * P], w_sb[:, s, c * P:(c + 1) * P], xt_sb[:, s % 2, :],
                              start=True, stop=True)
                last.then_inc(up_done, 1)

            def down(turn, s):
                pe.wait_ge(h_ready, turn * SLOTS + (s + 1 + BUFS))
                pe.wait_ge(y_ready, turn * SLOTS + (s + 1))
                for c in range(HC):
                    last = mm(down_ps[s % 2][:, 0:D], h_sb[:, s % 2, c, :], w_sb[:, s, H + c * D:H + (c + 1) * D],
                              start=(c == 0), stop=(c == HC - 1))
                last.then_inc(down_done, 1)

            with pe.Fori(0, OCTETS) as turn:
                for half in range(2):
                    o = half * QUAD
                    with pe.If(turn * 2 + half < quads):
                        turn_x(turn, o)
                        turn_x(turn, o + 1)
                        up(turn, o)
                        turn_x(turn, o + 2)
                        up(turn, o + 1)
                        down(turn, o)
                        turn_x(turn, o + 3)
                        up(turn, o + 2)
                        down(turn, o + 1)
                        up(turn, o + 3)
                        down(turn, o + 2)
                        down(turn, o + 3)


def kernel(x, adj, L0_gnn_kernel, L0_gnn_bias, L0_gnn_beta, L0_ffn_Wr, L0_ffn_br, L0_ffn_W1, L0_ffn_b1, L0_ffn_W2, L0_ffn_b2):
    import concourse.bacc as bacc
    from concourse.bass_utils import run_bass_kernel_spmd

    a = np.asarray
    adj_t = a(adj).reshape(GROUPS, GN, CHUNKS, CJ, P).transpose(0, 2, 4, 3, 1)
    w1 = a(L0_ffn_W1)
    w2 = a(L0_ffn_W2).reshape(E, HC, P, D).transpose(0, 2, 1, 3).reshape(E, P, HC * D)
    b1 = a(L0_ffn_b1).reshape(E, HC, P).transpose(0, 2, 1)
    arrays = {
        "x": a(x), "adj_t": adj_t, "gnn_w": a(L0_gnn_kernel), "gnn_b": a(L0_gnn_bias),
        "beta": a(L0_gnn_beta).reshape(TILES, P).T, "wr": a(L0_ffn_Wr), "br": a(L0_ffn_br),
        "w_pack": np.concatenate([w1, w2, b1], axis=2), "b2": a(L0_ffn_b2),
    }
    arrays = {name: np.ascontiguousarray(v) for name, v in arrays.items()}
    nc = bacc.Bacc("TRN2", target_bir_lowering=False, num_devices=1)
    args = [nc.dram_tensor(name, v.shape, mybir.dt.from_np(v.dtype), kind="ExternalInput").ap() for name, v in arrays.items()]
    out = nc.dram_tensor("out", [N, D], F32, kind="ExternalOutput").ap()
    program(nc, *args, out)
    result = run_bass_kernel_spmd(nc, [arrays], core_ids=[0])
    return result.results[0]["out"]
```

```python
from contextlib import ExitStack, nullcontext

import numpy as np

import concourse.bass as bass
from concourse import mybir

ALU = mybir.AluOpType
ACT = mybir.ActivationFunctionType
AX_X = mybir.AxisListType.X
F32 = mybir.dt.float32
BF16 = mybir.dt.bfloat16
I32 = mybir.dt.int32
U32 = mybir.dt.uint32

P = 128
N = 4096
D = 128
H = 256
E = 64
K = 2
EPS = 1e-5
HC = H // P
TILES = N // P
GT = 4
GN = GT * P
GROUPS = N // GN
CJ = 4
CHUNKS = TILES // CJ
ROW = D + 4
ANSWER = D
EXPERT_ROWS = N
NO_ANSWER = 1 << 20
SKIP = 1 << 21
WCOLS = H + HC * D + HC
QUAD = 4
SLOTS = 8
TILE_CAP = N * K // P + E
OCTETS = TILE_CAP // SLOTS
OUT_CH = 4
OUT_STEPS = TILES // OUT_CH


def lone_wait(eng, semaphore, value, passed):
    eng.wait_ge(semaphore, value)
    eng.sem_inc(passed, 1)


class Steps:

    def __init__(self, eng, sem):
        self.eng, self.sem, self.n, self.turn, self.per, self.start = eng, sem, 0, None, 0, 0

    def after(self, instruction, passed=None):
        instruction.then_inc(self.sem, 1)
        self.n += 1
        if passed is None:
            self.eng.wait_ge(self.sem, self.value())
        else:
            lone_wait(self.eng, self.sem, self.value(), passed)

    def value(self):
        if self.turn is None:
            return self.n
        return self.turn * self.per + self.n

    def enter(self, turn, per):
        self.turn, self.per, self.start = turn, per, self.n

    def leave(self, turns):
        assert self.n - self.start == self.per, (self.n - self.start, self.per)
        self.turn, self.n = None, self.start + self.per * turns


def program(nc, x, adj_t, gnn_w, gnn_b, beta, wr, br, w_pack, b2, out):
    rows = nc.dram_tensor("dispatched_rows", [E * EXPERT_ROWS, ROW], F32).ap()
    y_tok = nc.dram_tensor("expert_answers", [N * K, D], F32).ap()
    with ExitStack() as ctx:
        def sb(name, shape, dt=F32):
            return ctx.enter_context(nc.sbuf_tensor(name, shape, dt))

        def sem(name):
            return ctx.enter_context(nc.semaphore(name))

        bank = [ctx.enter_context(nc.psum_tensor(f"bank{i}", [P, 512], F32)) for i in range(8)]
        agg_ps = [bank[0], bank[1]]
        gnn_ps = bank[2][:].rearrange("p (t f) -> p t f", t=GT)
        turn_ps = bank[3]
        logit_ps = bank[4][:, 0:GT * E].rearrange("p (t e) -> p t e", t=GT)
        deg_ps = bank[4][:, GT * E:GT * E + GT]
        rank_ps = bank[5][:, 0:GT * E].rearrange("p (t e) -> p t e", t=GT)
        xt_ps = [bank[6], bank[7]]
        up_ps = [bank[0], bank[1]]
        down_ps = [bank[2], bank[3]]
        last_ps = bank[5]

        adj_sb = sb("adj_ring", [P, CHUNKS, CJ, GN])
        x_sb = sb("x_sb", [P, TILES, D])
        z_sb = sb("z_sb", [P, TILES, D])
        gnn_w_sb = sb("gnn_w_sb", [P, D])
        gnn_wd = sb("gnn_w_less_last_row", [P, D])
        gnn_b_sb = sb("gnn_b_sb", [P, D])
        wr_sb = sb("wr_sb", [P, E])
        br_sb = sb("br_sb", [P, E])
        b2_sb = sb("b2_sb", [E, D])
        beta_sb = sb("beta_sb", [P, TILES])
        ident = sb("ident", [P, P])
        last_row = sb("last_row", [P, P])
        before = sb("before", [P, P], BF16)
        ones_b = sb("ones_b", [P, P], BF16)
        ones_f = sb("ones_f", [P, P])
        iota_e = sb("iota_e", [P, E])
        iota_row = sb("iota_row", [P, P])
        iota_part = sb("iota_part", [P, 1])
        answer_tab = sb("answer_tab", [P, TILES, K])
        eps_sb = sb("eps_sb", [P, 1])
        pad_row = sb("pad_row", [P, ROW])
        stats = sb("stats", [P, GT, 6])
        mv = sb("mv", [P, GT, 2])
        std = sb("std", [P, GT])
        rstd = sb("rstd", [P, GT])
        zi = sb("zi", [P, GT, D])
        diag = sb("diag", [P, GT, P])
        agg_sb = sb("agg_sb", [P, GN])
        scale = sb("scale", [P, GT])
        x1 = sb("x1", [P, GT, D])
        payload = sb("payload", [P, GT, K, ROW])
        z1t = sb("z1t", [P, GN])
        logits = sb("logits", [P, GT, E])
        top = sb("top", [P, GT, 8])
        top_i = sb("top_i", [P, GT, 8], U32)
        chosen = sb("chosen", [P, GT, K])
        hot = sb("hot", [P, GT, K, E])
        mask = sb("mask", [P, GT, E], BF16)
        seen = sb("seen", [P, E], BF16)
        more = sb("more", [P, E])
        diff = sb("diff", [P, GT])
        ex = sb("ex", [P, GT])
        den = sb("den", [P, GT])
        gates = sb("gates", [P, TILES, K])
        work = sb("work", [P, GT, K, E])
        rank = sb("rank", [P, GT * K])
        slot = sb("slot", [P, GT * K], I32)
        comb = sb("comb", [P, GT, E])
        combt = sb("combt", [E, GN])
        cnt = sb("cnt", [P, E])
        cnt_i = sb("cnt_i", [P, E], I32)
        tiles_i = sb("tiles_i", [P, E], I32)
        tiles_f = sb("tiles_f", [P, E])
        upto = sb("upto", [P, E])
        past = sb("past", [P, E])
        lw = sb("lw", [P, E])
        lc = sb("lc", [P, 16])
        lst = sb("lst", [P, 2])
        q_i = sb("q_i", [P, 2], I32)
        ov_diag = sb("ov_diag", [P, P])
        skip_tab = sb("skip_tab", [P, P])
        table = sb("table", [2, P], I32)
        w_sb = sb("w_sb", [P, SLOTS, WCOLS])
        xin = sb("xin", [P, SLOTS, ROW])
        xt_sb = sb("xt_sb", [P, 2, P])
        h_sb = sb("h_sb", [P, 2, HC, P])
        y_sb = sb("y_sb", [P, SLOTS, D])
        ans = sb("ans", [P, SLOTS], I32)
        y_in = sb("y_in", [P, TILES, K, D])
        o_sb = sb("o_sb", [P, TILES, D])

        x_first = sem("x_first")
        x_in = sem("x_in")
        params_in = sem("params_in")
        adj_in = [sem(f"adj_in{k}") for k in range(CHUNKS)]
        prefilled = sem("prefilled")
        consts = sem("consts")
        passed = sem("passed")
        pool_own = sem("pool_own")
        dve_own = sem("dve_own")
        act_own = sem("act_own")
        var0 = sem("var0")
        std0 = sem("std0")
        z_ready = sem("z_ready")
        bias_added = sem("bias_added")
        wrow_done = sem("wrow_done")
        wd_ready = sem("wd_ready")
        chunk_used = sem("chunk_used")
        own_ready = sem("own_ready")
        agg_done = sem("agg_done")
        agg_copied = sem("agg_copied")
        gnn_done = sem("gnn_done")
        var1 = sem("var1")
        std1 = sem("std1")
        z1_ready = sem("z1_ready")
        z1_turned = sem("z1_turned")
        z1t_ready = sem("z1t_ready")
        logits_done = sem("logits_done")
        mask_ready = sem("mask_ready")
        seen_ready = sem("seen_ready")
        rank_done = sem("rank_done")
        diff_ready = sem("diff_ready")
        ex_ready = sem("ex_ready")
        slots_ready = sem("slots_ready")
        payload_free = sem("payload_free")
        scattered = sem("scattered")
        comb_ready = sem("comb_ready")
        comb_turned = sem("comb_turned")
        combt_ready = sem("combt_ready")
        b2_done = sem("b2_done")
        base_ready = sem("base_ready")
        total_ready = sem("total_ready")
        total_done = sem("total_done")
        list_ready = sem("list_ready")
        list_turned = sem("list_turned")
        table_ready = sem("table_ready")
        tile_in = [sem(f"tile_in{s}") for s in range(SLOTS)]
        x_turned = sem("x_turned")
        xt_ready = sem("xt_ready")
        up_done = sem("up_done")
        h_ready = sem("h_ready")
        down_done = sem("down_done")
        y_ready = sem("y_ready")
        y_out = [sem(f"y_out{s}") for s in range(SLOTS)]
        y_back = [sem(f"y_back{c}") for c in range(OUT_STEPS)]
        o_ready = sem("o_ready")
        stored = sem("stored")

        BUFS = 2

        def quads_in_use(eng):
            return eng.value_load(table[1:2, 0:1], min_val=TILE_CAP // 2 // QUAD, max_val=TILE_CAP // QUAD)

        def ahead(eng, turn, half, quads, three, two, now):
            for s in range(half * QUAD, half * QUAD + QUAD):
                end = half * QUAD + QUAD

                def step(which, n):
                    if n < SLOTS:
                        which(turn, n)
                    else:
                        which(turn + 1, n - SLOTS)

                if s + 3 < end:
                    step(three, s + 3)
                    if two:
                        step(two, s + 2)
                else:
                    if two and s + 2 < end:
                        step(two, s + 2)
                    with nullcontext() if quads is None else eng.If(turn * 2 + (half + 1) < quads):
                        step(three, s + 3)
                        if two and s + 2 >= end:
                            step(two, s + 2)
                now(turn, s)

        block = ctx.enter_context(nc.Block())

        @block.sync
        def _(sp):
            x_tiles = x.rearrange("(t p) f -> p t f", p=P)
            sp.dma_start(x_sb[:, 0:GT], x_tiles[:, 0:GT]).then_inc(x_first, 16)

            def load_chunk(g, k):
                sp.dma_start(adj_sb[:, k], adj_t[g, k] if isinstance(g, int) else adj_t[bass.ds(g, 1), k].rearrange("a p u n -> (a p) u n")).then_inc(adj_in[k], 16)

            for k in range(CHUNKS):
                load_chunk(0, k)
                if k == 0:
                    sp.dma_start(x_sb[:, GT:TILES], x_tiles[:, GT:TILES]).then_inc(x_in, 16)
                if k == 1:
                    sp.dma_start(gnn_w_sb[:], gnn_w).then_inc(params_in, 16)
                    sp.dma_start(beta_sb[:], beta).then_inc(params_in, 16)
                    sp.dma_start(gnn_b_sb[:], gnn_b.partition_broadcast(P)).then_inc(params_in, 16)
                    sp.dma_start(wr_sb[:], wr).then_inc(params_in, 16)
                    sp.dma_start(br_sb[:], br.partition_broadcast(P)).then_inc(params_in, 16)
                    sp.dma_start(b2_sb[:], b2).then_inc(params_in, 16)
            sp.wait_ge(consts, 1)
            sp.dma_start(rows.rearrange("(e s) c -> s e c", e=E)[0:P],
                         pad_row[:, None, :].to_broadcast([P, E, ROW])).then_inc(prefilled, 16)
            with sp.Fori(1, GROUPS) as g:
                for k in range(CHUNKS):
                    sp.wait_ge(chunk_used, g * CHUNKS + (k + 1 - CHUNKS))
                    load_chunk(g, k)

            def load_quad(starts, slot0, turn):
                for s in range(slot0, slot0 + QUAD):
                    start = starts[s]
                    if turn is not None:
                        sp.wait_ge(y_ready, turn * SLOTS + (s + 1 + BUFS))
                    sp.dma_start(w_sb[:, s], w_pack[bass.ds(start // EXPERT_ROWS, 1)].rearrange("a p c -> (a p) c")).then_inc(tile_in[s], 16)
                    if turn is None and s == 0:
                        sp.wait_ge(scattered, 16 * TILES * K)
                    sp.dma_start(xin[:, s], rows[bass.ds(start, P), :]).then_inc(tile_in[s], 16)

            def load_starts(octet, octets):
                return nc.values_load_multi_w_load_instructions(
                    table[0:1, bass.ds(octet * SLOTS, octets * SLOTS)], engines=[mybir.EngineType.SP],
                    min_val=0, max_val=E * EXPERT_ROWS - P)[1]

            sp.wait_ge(table_ready, 1)
            quads = quads_in_use(sp)
            starts = load_starts(0, 2)
            load_quad(starts, 0, None)
            load_quad(starts, QUAD, None)
            load_quad(starts[SLOTS:], 0, 0)
            load_quad(starts[SLOTS:], QUAD, 0)
            with sp.Fori(1, OCTETS // 2) as pair:
                with sp.If(pair * 4 < quads):
                    starts = load_starts(pair * 2, 2)
                    load_quad(starts, 0, pair * 2 - 1)
                    for half in range(1, 4):
                        with sp.If(pair * 4 + half < quads):
                            load_quad(starts[half // 2 * SLOTS:], half % 2 * QUAD, pair * 2 + (half // 2 - 1))
            for s in range(SLOTS):
                sp.wait_ge(y_out[s], ((quads + (1 if s < QUAD else 0)) // 2) * 16)
            answers = y_tok.rearrange("(t p k) f -> p t k f", p=P, k=K)
            for c in range(OUT_STEPS):
                sp.dma_start(y_in[:, c * OUT_CH:(c + 1) * OUT_CH], answers[:, c * OUT_CH:(c + 1) * OUT_CH]).then_inc(y_back[c], 16)
            for c in range(OUT_STEPS):
                sp.wait_ge(o_ready, c + 1)
                sp.dma_start(out.rearrange("(t p) f -> p t f", p=P)[:, c * OUT_CH:(c + 1) * OUT_CH],
                             o_sb[:, c * OUT_CH:(c + 1) * OUT_CH]).then_inc(stored, 16)
            sp.wait_ge(stored, 16 * OUT_STEPS)

        @block.gpsimd
        def _(pool):
            own = Steps(pool, pool_own)
            pool.memset(pad_row[:], 0.0)
            pool.memset(ident[:], 0.0)
            pool.memset(last_row[:], 0.0)
            pool.memset(before[:], 0.0)
            pool.memset(ones_b[:], 1.0)
            pool.memset(ones_f[:], 1.0)
            pool.memset(seen[:], 0.0)
            pool.memset(eps_sb[:], EPS)
            own.after(pool.memset(payload[:], 0.0))
            pool.memset(pad_row[:, ANSWER:ANSWER + 1], float(NO_ANSWER))
            pool.affine_select(out=ident[:], in_=ident[:], compare_op=ALU.not_equal, fill=1.0, base=0,
                               pattern=[[-1, P]], channel_multiplier=1)
            pool.affine_select(out=last_row[:], in_=last_row[:], compare_op=ALU.not_equal, fill=1.0, base=1 - P,
                               pattern=[[0, P]], channel_multiplier=1)
            pool.affine_select(out=before[:], in_=before[:], compare_op=ALU.is_ge, fill=1.0, base=0,
                               pattern=[[-1, P]], channel_multiplier=1)
            pool.iota(iota_e[:], [[1, E]], base=0, channel_multiplier=0, allow_small_or_imprecise_dtypes=True)
            pool.iota(iota_row[:], [[1, P]], base=0, channel_multiplier=0, allow_small_or_imprecise_dtypes=True)
            pool.iota(iota_part[:], [[0, 1]], base=0, channel_multiplier=1, allow_small_or_imprecise_dtypes=True)
            pool.iota(answer_tab[:], [[P * K, TILES], [1, K]], base=0, channel_multiplier=K,
                      allow_small_or_imprecise_dtypes=True)
            own.after(pool.memset(z_sb[:, :, D - 1:D], 1.0))
            pool.sem_inc(consts, 1)
            pool.sem_inc(payload_free, 1)
            pool.wait_ge(params_in, 16 * 6)
            own.enter(None, 0)
            with pool.Fori(0, GROUPS) as c:
                lone_wait(pool, z_ready, c * GT + GT, passed)
                xs = x_sb[:, bass.ds(c * GT, GT), :]
                pool.tensor_tensor(xs, xs, gnn_b_sb[:, None, :].to_broadcast([P, GT, D]), ALU.add).then_inc(bias_added, 1)

            def own_rows(tiles):
                pool.tensor_copy(zi[:], z_sb[:, tiles, :])
                pool.tensor_tensor(diag[:], ident[:, None, :].to_broadcast([P, GT, P]),
                                   beta_sb[:, tiles].to_broadcast([P, GT, P]), ALU.mult).then_inc(own_ready, 1)

            def dispatch(g):
                lone_wait(pool, z1_ready, g + 1, passed)
                pool.tensor_copy(payload[:, :, 1, 0:D], payload[:, :, 0, 0:D]).then_inc(pool_own, 1)
                pool.tensor_copy(payload[:, :, :, ANSWER], answer_tab[:, bass.ds(g * GT, GT), :]).then_inc(pool_own, 1)
                lone_wait(pool, pool_own, g * 2 + (own.n + 2), passed)
                pool.wait_ge(prefilled, 16)
                lone_wait(pool, slots_ready, g + 1, passed)
                for t in range(GT):
                    for k in range(K):
                        i = t * K + k
                        pool.indirect_dma_start(rows, bass.IndirectOffsetOnAxis(ap=slot[:, i:i + 1], axis=0),
                                                payload[:, t, k, :], None).then_inc(scattered, 16)
                pool.wait_ge(scattered, g * (GT * K * 16) + GT * K * 16)
                pool.sem_inc(payload_free, 1)

            own_rows(slice(0, GT))
            with pool.Fori(0, GROUPS - 1) as g:
                lone_wait(pool, agg_done, g + 2, passed)
                own_rows(bass.ds(g * GT + GT, GT))
                dispatch(g)
            dispatch(GROUPS - 1)

            pool.wait_ge(table_ready, 1)
            quads = quads_in_use(pool)
            with pool.Fori(0, OCTETS) as turn:
                for half in range(2):
                    with pool.If(turn * 2 + half < quads):
                        for s in range(half * QUAD, half * QUAD + QUAD):
                            lone_wait(pool, y_ready, turn * SLOTS + (s + 1 + BUFS), passed)
                            pool.indirect_dma_start(y_tok, bass.IndirectOffsetOnAxis(ap=ans[:, s:s + 1], axis=0),
                                                    y_sb[:, s, :], None, bounds_check=N * K - 1,
                                                    oob_is_err=False).then_inc(y_out[s], 16)

        @block.scalar
        def _(act):
            act.wait_ge(consts, 1)
            with act.Fori(0, GROUPS) as c:
                act.wait_ge(var0, c + 1)
                nc.scalar.activation(std[:], mv[:, :, 1], ACT.Sqrt, bias=eps_sb[:]).then_inc(std0, 1)
            with act.Fori(0, GROUPS // 2) as pair:
                for b in range(2):
                    g1 = pair * 2 + (b + 1)
                    act.wait_ge(agg_done, g1 + 1)
                    nc.scalar.copy(agg_sb[:], agg_ps[b][:]).then_inc(agg_copied, 1)
                    act.wait_ge(var1, g1)
                    nc.scalar.activation(std[:], mv[:, :, 1], ACT.Sqrt, bias=eps_sb[:]).then_inc(std1, 1)
                    act.wait_ge(z1_turned, g1)
                    nc.scalar.copy(z1t[:], turn_ps[:]).then_inc(z1t_ready, 1)
                    act.wait_ge(diff_ready, g1)
                    nc.scalar.activation(ex[:], diff[:], ACT.Exp).then_inc(ex_ready, 1)
                    act.wait_ge(comb_turned, g1)
                    nc.scalar.copy(combt[:], turn_ps[0:E, :]).then_inc(combt_ready, 1)
            act.sem_inc(h_ready, BUFS)
            act.wait_ge(table_ready, 1)
            quads = quads_in_use(act)
            with act.Fori(0, OCTETS) as turn:
                for half in range(2):
                    with act.If(turn * 2 + half < quads):
                        for s in range(half * QUAD, half * QUAD + QUAD):
                            act.wait_ge(up_done, turn * SLOTS + (s + 1 + BUFS))
                            act.wait_ge(down_done, turn * SLOTS + (s + 1))
                            for c in range(HC):
                                last = nc.scalar.activation(h_sb[:, s % 2, c, :], up_ps[s % 2][:, c * P:(c + 1) * P],
                                                            ACT.Relu, bias=w_sb[:, s, H + HC * D + c:H + HC * D + c + 1])
                            last.then_inc(h_ready, 1)

        @block.vector
        def _(dve):
            own = Steps(dve, dve_own)
            v = nc.vector
            dve.wait_ge(consts, 1)
            dve.wait_ge(x_first, 16)
            def norm_x(c):
                for t in range(GT):
                    last = v.bn_stats(stats[:, t, :], x_sb[:, bass.ds(c * GT + t, 1), :].rearrange("p a f -> p (a f)"))
                own.after(last, passed)
                for t in range(GT):
                    last = v.bn_aggr(mv[:, t, :], stats[:, t, :])
                last.then_inc(var0, 1)
                dve.wait_ge(std0, c + 1)
                own.after(v.reciprocal(rstd[:], std[:]))
                for t in range(GT):
                    xs = x_sb[:, bass.ds(c * GT + t, 1), 0:D - 1].rearrange("p a f -> p (a f)")
                    zs = z_sb[:, bass.ds(c * GT + t, 1), 0:D - 1].rearrange("p a f -> p (a f)")
                    v.tensor_scalar(zs, xs, mv[:, t, 0:1], rstd[:, t:t + 1], ALU.subtract, ALU.mult).then_inc(z_ready, 1)
                dve.wait_ge(z_ready, c * GT + GT)

            norm_x(0)
            dve.wait_ge(x_in, 16)
            with dve.Fori(1, GROUPS) as c:
                own.enter(c - 1, 2)
                norm_x(c)
                own.leave(GROUPS - 1)
            dve.wait_ge(wrow_done, 1)
            v.tensor_tensor(gnn_wd[:], gnn_w_sb[:], bank[6][:, 0:D], ALU.subtract).then_inc(wd_ready, 1)
            dve.sem_inc(base_ready, 1)

            with dve.Fori(0, GROUPS) as g:
                own.enter(g, 17)
                dve.wait_ge(bias_added, g + 1)
                dve.wait_ge(gnn_done, g + 1)
                own.after(v.reciprocal(scale[:], deg_ps))
                own.after(v.tensor_tensor(x1[:], gnn_ps, scale[:].to_broadcast([P, GT, D]), ALU.mult))
                own.after(v.tensor_tensor(x1[:], x1[:], x_sb[:, bass.ds(g * GT, GT), :], ALU.add))
                for t in range(GT):
                    last = v.bn_stats(stats[:, t, :], x1[:, t, :])
                own.after(last, passed)
                for t in range(GT):
                    last = v.bn_aggr(mv[:, t, :], stats[:, t, :])
                last.then_inc(var1, 1)
                dve.wait_ge(std1, g + 1)
                own.after(v.reciprocal(rstd[:], std[:]))
                dve.wait_ge(payload_free, g + 1)
                for t in range(GT):
                    last = v.tensor_scalar(payload[:, t, 0, 0:D], x1[:, t, :], mv[:, t, 0:1], rstd[:, t:t + 1],
                                           ALU.subtract, ALU.mult)
                last.then_inc(z1_ready, 1)
                dve.wait_ge(logits_done, g + 1)
                own.after(v.tensor_tensor(logits[:], logit_ps, br_sb[:, None, :].to_broadcast([P, GT, E]), ALU.add), passed)
                for t in range(GT):
                    last = v.max(top[:, t, :], logits[:, t, :])
                own.after(last, passed)
                for t in range(GT):
                    last = v.max_index(top_i[:, t, :], top[:, t, :], logits[:, t, :])
                own.after(last)
                v.tensor_tensor(diff[:], top[:, :, 1], top[:, :, 0], ALU.subtract).then_inc(diff_ready, 1)
                own.after(v.tensor_copy(chosen[:], top_i[:, :, 0:K]))
                own.after(v.tensor_tensor(hot[:].rearrange("p t k e -> p (t k) e"),
                                          iota_e[:, None, :].to_broadcast([P, GT * K, E]),
                                          chosen[:].rearrange("p t k -> p (t k)").to_broadcast([P, GT * K, E]), ALU.is_equal))
                v.tensor_tensor(mask[:], hot[:, :, 0, :], hot[:, :, 1, :], ALU.add).then_inc(mask_ready, 1)
                dve.wait_ge(ex_ready, g + 1)
                own.after(v.tensor_scalar(den[:], ex[:], 1.0, None, ALU.add))
                gs = gates[:, bass.ds(g * GT, GT), :]
                own.after(v.reciprocal(den[:], den[:]))
                v.tensor_copy(gs[:, :, 0], den[:])
                own.after(v.tensor_tensor(gs[:, :, 1], ex[:], den[:], ALU.mult))
                dve.wait_ge(rank_done, g + 1)
                for k in range(K):
                    last = v.tensor_tensor(work[:, :, k, :], hot[:, :, k, :], rank_ps, ALU.mult)
                own.after(last)
                own.after(v.tensor_reduce(more[:], mask[:].rearrange("p t e -> p e t"), AX_X, ALU.add))
                v.tensor_tensor(seen[:], seen[:], more[:], ALU.add).then_inc(seen_ready, 1)
                own.after(v.tensor_reduce(rank[:], work[:].rearrange("p t k e -> p (t k) e"), AX_X, ALU.add))
                v.scalar_tensor_tensor(out=slot[:], in0=chosen[:].rearrange("p t k -> p (t k)"), scalar=float(EXPERT_ROWS),
                                       in1=rank[:], op0=ALU.mult, op1=ALU.add).then_inc(slots_ready, 1)
                own.after(v.tensor_tensor(work[:].rearrange("p t k e -> p (t k) e"), hot[:].rearrange("p t k e -> p (t k) e"),
                                          gs.rearrange("p t k -> p (t k)").to_broadcast([P, GT * K, E]), ALU.mult))
                v.tensor_tensor(comb[:], work[:, :, 0, :], work[:, :, 1, :], ALU.add).then_inc(comb_ready, 1)
                dve.wait_ge(b2_done, g + 1)
                v.tensor_tensor(x_sb[:, bass.ds(g * GT, GT), :], gnn_ps, x1[:], ALU.add).then_inc(base_ready, 1)
                own.leave(GROUPS)

            dve.wait_ge(total_done, 1)
            own.after(v.tensor_copy(cnt[:], last_ps[:, 0:E]))
            own.after(v.tensor_scalar(cnt_i[:], cnt[:], float(P - 1), None, ALU.add))
            own.after(v.tensor_scalar(tiles_i[:], cnt_i[:], 7, None, ALU.logical_shift_right))
            own.after(v.tensor_copy(tiles_f[:], tiles_i[:]))
            own.after(v.tensor_tensor_scan(upto[:], tiles_f[:], ones_f[:, 0:E], 0.0, ALU.add, ALU.mult))
            used = upto[:, E - 1:E]
            own.after(v.tensor_scalar(past[:], upto[:], iota_part[:], None, ALU.is_le))
            own.after(v.tensor_reduce(lc[:, 0:1], past[:], AX_X, ALU.add))
            own.after(v.tensor_tensor(lw[:], past[:], upto[:], ALU.mult))
            own.after(v.tensor_reduce(lc[:, 1:2], lw[:], AX_X, ALU.max))
            own.after(v.tensor_scalar(past[:], iota_e[:], lc[:, 0:1], None, ALU.is_equal))
            own.after(v.tensor_tensor(lw[:], past[:], cnt[:], ALU.mult))
            own.after(v.tensor_reduce(lc[:, 2:3], lw[:], AX_X, ALU.add))
            own.after(v.tensor_tensor(lc[:, 3:4], iota_part[:], lc[:, 1:2], ALU.subtract))
            own.after(v.tensor_scalar(lc[:, 3:4], lc[:, 3:4], float(P), None, ALU.mult))
            own.after(v.tensor_scalar(lc[:, 4:5], lc[:, 2:3], float(-P), 0.0, ALU.add, ALU.max))
            own.after(v.tensor_tensor(lc[:, 5:6], lc[:, 3:4], lc[:, 4:5], ALU.min))
            own.after(v.tensor_tensor(lc[:, 6:7], lc[:, 3:4], lc[:, 5:6], ALU.subtract))
            own.after(v.tensor_tensor(lc[:, 7:8], iota_part[:], used, ALU.is_lt))
            own.after(v.scalar_tensor_tensor(out=lc[:, 8:9], in0=lc[:, 0:1], scalar=float(EXPERT_ROWS), in1=lc[:, 5:6],
                                             op0=ALU.mult, op1=ALU.add))
            v.tensor_tensor(lst[:, 0:1], lc[:, 8:9], lc[:, 7:8], ALU.mult)
            own.after(v.tensor_scalar(lc[:, 9:10], lc[:, 6:7], float(-P), lc[:, 7:8], ALU.add, ALU.mult))
            own.after(v.tensor_scalar(lc[:, 10:11], lc[:, 9:10], float(P), None, ALU.add))
            own.after(v.tensor_scalar(q_i[:, 0:1], used, float(QUAD - 1), None, ALU.add))
            own.after(v.tensor_scalar(q_i[:, 1:2], q_i[:, 0:1], 2, None, ALU.logical_shift_right))
            v.tensor_copy(lst[:, 1:2], q_i[:, 1:2])
            own.after(v.tensor_scalar(ov_diag[:], ident[:], lc[:, 10:11], None, ALU.mult))
            dve.sem_inc(list_ready, 1)
            dve.wait_ge(list_turned, 1)
            own.after(v.tensor_copy(table[:], bank[6][0:2, 0:P]))
            own.after(v.tensor_scalar(skip_tab[:], bank[6][:, P:2 * P], iota_part[:], float(SKIP), ALU.is_gt, ALU.mult))
            dve.sem_inc(table_ready, 1)
            dve.sem_inc(xt_ready, BUFS)
            dve.sem_inc(y_ready, BUFS)

            quads = quads_in_use(dve)

            def copy_xt(turn, s):
                dve.wait_ge(x_turned, turn * SLOTS + (s + 1 + BUFS))
                dve.wait_ge(up_done, turn * SLOTS + (s + 1))
                v.tensor_copy(xt_sb[:, s % 2, :], xt_ps[s % 2][:, 0:P]).then_inc(xt_ready, 1)

            def copy_y(turn, s):
                if not isinstance(turn, int):
                    dve.wait_ge(y_out[s], turn * 16)
                v.tensor_tensor(ans[:, s:s + 1], xin[:, s, ANSWER:ANSWER + 1],
                                skip_tab[:, bass.ds(turn * SLOTS + s, 1)], ALU.add)
                dve.wait_ge(down_done, turn * SLOTS + (s + 1 + BUFS))
                v.tensor_copy(y_sb[:, s, :], down_ps[s % 2][:, 0:D]).then_inc(y_ready, 1)

            for s in range(3):
                copy_xt(0, s)
            for half in range(2):
                ahead(dve, 0, half, None, copy_xt, None, copy_y)
            with dve.Fori(1, OCTETS) as turn:
                for half in range(2):
                    with dve.If(turn * 2 + half < quads):
                        ahead(dve, turn, half, quads, copy_xt, None, copy_y)

            per = OUT_CH
            for c in range(OUT_STEPS):
                dve.wait_ge(y_back[c], 16)
                for t in range(c * per, (c + 1) * per):
                    v.scalar_tensor_tensor(out=o_sb[:, t, :], in0=y_in[:, t, 0, :], scalar=gates[:, t, 0:1],
                                           in1=x_sb[:, t, :], op0=ALU.mult, op1=ALU.add).then_inc(dve_own, 1)
                    own.n += 1
                for t in range(c * per, (c + 1) * per):
                    dve.wait_ge(dve_own, own.n - per + 1 + t - c * per)
                    last = v.scalar_tensor_tensor(out=o_sb[:, t, :], in0=y_in[:, t, 1, :], scalar=gates[:, t, 1:2],
                                                  in1=o_sb[:, t, :], op0=ALU.mult, op1=ALU.add)
                last.then_inc(o_ready, 1)

        @block.tensor
        def _(pe):
            mm = nc.tensor.matmul
            pe.wait_ge(consts, 1)
            pe.sem_inc(agg_done, 1)

            def gnn(g):
                pe.wait_ge(wd_ready, 1)
                pe.wait_ge(base_ready, g + 1)
                pe.wait_ge(agg_copied, g + 1)
                for t in range(GT):
                    mm(gnn_ps[:, t, :], agg_sb[:, t * P:(t + 1) * P], gnn_wd[:], start=True, stop=True)
                for t in range(GT):
                    last = mm(deg_ps[:, t:t + 1], agg_sb[:, t * P:(t + 1) * P], last_row[:, 0:1], start=True, stop=True)
                last.then_inc(gnn_done, 1)

            def turn_z1(g):
                pe.wait_ge(z1_ready, g + 1)
                for t in range(GT):
                    last = nc.tensor.transpose(turn_ps[:, t * P:(t + 1) * P], payload[:, t, 0, 0:D], ident[:])
                last.then_inc(z1_turned, 1)

            def router(g):
                pe.wait_ge(z1t_ready, g + 1)
                for t in range(GT):
                    last = mm(logit_ps[:, t, :], z1t[:, t * P:(t + 1) * P], wr_sb[:], start=True, stop=True)
                last.then_inc(logits_done, 1)

            def ranks(g):
                pe.wait_ge(mask_ready, g + 1)
                mm(rank_ps, before[:], mask[:], start=True, stop=False)
                mm(rank_ps, ones_b[:], seen[:, None, :].to_broadcast([P, GT, E]), start=False, stop=False)
                for t in range(1, GT):
                    last = mm(rank_ps[:, t:GT, :], ones_b[:], mask[:, t - 1:t, :].to_broadcast([P, GT - t, E]),
                              start=False, stop=(t == GT - 1))
                last.then_inc(rank_done, 1)

            def turn_comb(g):
                lone_wait(pe, comb_ready, g + 1, passed)
                for t in range(GT):
                    last = nc.tensor.transpose(turn_ps[0:E, t * P:(t + 1) * P], comb[:, t, :], ident[:])
                last.then_inc(comb_turned, 1)

            def bias2(g):
                pe.wait_ge(combt_ready, g + 1)
                for t in range(GT):
                    last = mm(gnn_ps[:, t, :], combt[:, t * P:(t + 1) * P], b2_sb[:], start=True, stop=True)
                last.then_inc(b2_done, 1)

            later = {2: gnn, 11: turn_z1, 14: router, 20: ranks, 26: turn_comb, 29: bias2}

            def aggregate(g, b, prev):
                for j in range(TILES):
                    if j % CJ == 0:
                        pe.wait_ge(adj_in[j // CJ], g * 16 + 16)
                    if prev is None:
                        pe.wait_ge(z_ready, j + 1)
                    elif j in later:
                        later[j](prev)
                    last = mm(agg_ps[b][:], z_sb[:, j, :], adj_sb[:, j // CJ, j % CJ, :], start=(j == 0), stop=False)
                    if j % CJ == CJ - 1:
                        last.then_inc(chunk_used, 1)
                pe.wait_ge(own_ready, g + 1)
                for t in range(GT):
                    last = mm(agg_ps[b][:, t * P:(t + 1) * P], zi[:, t, :], diag[:, t, :], start=False, stop=(t == GT - 1))
                last.then_inc(agg_done, 1)

            aggregate(0, 0, None)
            pe.wait_ge(params_in, 16 * 6)
            mm(bank[6][:, 0:D], last_row[:], gnn_w_sb[:], start=True, stop=True).then_inc(wrow_done, 1)
            with pe.Fori(0, GROUPS // 2 - 1) as i:
                aggregate(i * 2 + 1, 1, i * 2)
                aggregate(i * 2 + 2, 0, i * 2 + 1)
            aggregate(GROUPS - 1, 1, GROUPS - 2)
            for step in later.values():
                step(GROUPS - 1)
                if step is ranks:
                    pe.wait_ge(seen_ready, GROUPS)
                    mm(last_ps[:, 0:E], ones_b[:], seen[:], start=True, stop=True).then_inc(total_done, 1)
            pe.wait_ge(list_ready, 1)
            nc.tensor.transpose(bank[6][0:2, 0:P], lst[:], ident[:])
            mm(bank[6][:, P:2 * P], ones_f[:], ov_diag[:], start=True, stop=True).then_inc(list_turned, 1)

            pe.wait_ge(table_ready, 1)
            pe.wait_ge(base_ready, GROUPS + 1)
            pe.sem_inc(x_turned, BUFS)
            pe.sem_inc(up_done, BUFS)
            pe.sem_inc(down_done, BUFS)
            quads = quads_in_use(pe)

            def turn_x(turn, s):
                pe.wait_ge(tile_in[s], turn * 32 + 32)
                pe.wait_ge(xt_ready, turn * SLOTS + (s + 1))
                nc.tensor.transpose(xt_ps[s % 2][:, 0:P], xin[:, s, 0:D], ident[:]).then_inc(x_turned, 1)

            def up(turn, s):
                pe.wait_ge(xt_ready, turn * SLOTS + (s + 1 + BUFS))
                pe.wait_ge(h_ready, turn * SLOTS + (s + 1))
                for c in range(HC):
                    last = mm(up_ps[s % 2][:, c * P:(c + 1) * P], w_sb[:, s, c * P:(c + 1) * P], xt_sb[:, s % 2, :],
                              start=True, stop=True)
                last.then_inc(up_done, 1)

            def down(turn, s):
                pe.wait_ge(h_ready, turn * SLOTS + (s + 1 + BUFS))
                pe.wait_ge(y_ready, turn * SLOTS + (s + 1))
                for c in range(HC):
                    last = mm(down_ps[s % 2][:, 0:D], h_sb[:, s % 2, c, :], w_sb[:, s, H + c * D:H + (c + 1) * D],
                              start=(c == 0), stop=(c == HC - 1))
                last.then_inc(down_done, 1)

            turn_x(0, 0)
            turn_x(0, 1)
            up(0, 0)
            turn_x(0, 2)
            up(0, 1)
            with pe.Fori(0, OCTETS) as turn:
                for half in range(2):
                    with pe.If(turn * 2 + half < quads):
                        ahead(pe, turn, half, quads, turn_x, up, down)


def kernel(x, adj, L0_gnn_kernel, L0_gnn_bias, L0_gnn_beta, L0_ffn_Wr, L0_ffn_br, L0_ffn_W1, L0_ffn_b1, L0_ffn_W2, L0_ffn_b2):
    import concourse.bacc as bacc
    from concourse.bass_utils import run_bass_kernel_spmd

    a = np.asarray
    adj_t = a(adj).reshape(GROUPS, GN, CHUNKS, CJ, P).transpose(0, 2, 4, 3, 1)
    w1 = a(L0_ffn_W1)
    w2 = a(L0_ffn_W2).reshape(E, HC, P, D).transpose(0, 2, 1, 3).reshape(E, P, HC * D)
    b1 = a(L0_ffn_b1).reshape(E, HC, P).transpose(0, 2, 1)
    arrays = {
        "x": a(x), "adj_t": adj_t, "gnn_w": a(L0_gnn_kernel), "gnn_b": a(L0_gnn_bias),
        "beta": a(L0_gnn_beta).reshape(TILES, P).T, "wr": a(L0_ffn_Wr), "br": a(L0_ffn_br),
        "w_pack": np.concatenate([w1, w2, b1], axis=2), "b2": a(L0_ffn_b2),
    }
    arrays = {name: np.ascontiguousarray(v) for name, v in arrays.items()}
    nc = bacc.Bacc("TRN2", target_bir_lowering=False, num_devices=1)
    args = [nc.dram_tensor(name, v.shape, mybir.dt.from_np(v.dtype), kind="ExternalInput").ap() for name, v in arrays.items()]
    out = nc.dram_tensor("out", [N, D], F32, kind="ExternalOutput").ap()
    program(nc, *args, out)
    result = run_bass_kernel_spmd(nc, [arrays], core_ids=[0])
    return result.results[0]["out"]
```

```python
from contextlib import ExitStack, nullcontext

import numpy as np

import concourse.bass as bass
from concourse import mybir

ALU = mybir.AluOpType
ACT = mybir.ActivationFunctionType
AX_X = mybir.AxisListType.X
F32 = mybir.dt.float32
F32R = mybir.dt.float32r
BF16 = mybir.dt.bfloat16
I32 = mybir.dt.int32
U32 = mybir.dt.uint32

P = 128
N = 4096
D = 128
H = 256
E = 64
K = 2
EPS = 1e-5
HC = H // P
TILES = N // P
GT = 4
NT = 2 * GT
GN = GT * P
GROUPS = N // GN
CJ = 4
CHUNKS = TILES // CJ
ROW = D + 4
ANSWER = D
EC = E // 8
PADS = ((0, 0, 1, 0, 1, 0, 0, 1), (0, 1, 0, 1, 1, 1, 1, 0))
EXPERT_ROWS = N
NO_ANSWER = 1 << 20
SKIP = 1 << 21
WCOLS = H + HC * D + HC
QUAD = 4
SLOTS = 8
SP_SLOTS = 4
BUFS, DEEP = 2, 4
TILE_CAP = N * K // P + E
OCTETS = TILE_CAP // SLOTS
SPLIT = 6
PARTS = 3
ARRIVE = 3
RING = ARRIVE + CHUNKS - SPLIT
OUT_CH = 4
OUT_STEPS = TILES // OUT_CH


def lone_wait(eng, semaphore, value, passed):
    eng.wait_ge(semaphore, value)
    eng.sem_inc(passed, 1)


class Steps:

    def __init__(self, eng, sem):
        self.eng, self.sem, self.n, self.turn, self.per, self.start = eng, sem, 0, None, 0, 0

    def after(self, instruction, passed=None):
        instruction.then_inc(self.sem, 1)
        self.n += 1
        if passed is None:
            self.eng.wait_ge(self.sem, self.value())
        else:
            lone_wait(self.eng, self.sem, self.value(), passed)

    def value(self):
        if self.turn is None:
            return self.n
        return self.turn * self.per + self.n

    def enter(self, turn, per):
        self.turn, self.per, self.start = turn, per, self.n

    def leave(self, turns):
        assert self.n - self.start == self.per, (self.n - self.start, self.per)
        self.turn, self.n = None, self.start + self.per * turns


def program(nc, x, adj_t, gnn_w, gnn_b, beta, wr, br, w_pack, b2, out):
    rows = nc.dram_tensor("dispatched_rows", [E * EXPERT_ROWS, ROW], F32).ap()
    y_tok = nc.dram_tensor("expert_answers", [N * K, D], F32).ap()
    with ExitStack() as ctx:
        def sb(name, shape, dt=F32):
            return ctx.enter_context(nc.sbuf_tensor(name, shape, dt))

        def sem(name):
            return ctx.enter_context(nc.semaphore(name))

        bank = [ctx.enter_context(nc.psum_tensor(f"bank{i}", [P, 512], F32)) for i in range(8)]
        agg_ps = [bank[0], bank[1]]
        gnn_ps = bank[2][:].rearrange("p (t f) -> p t f", t=GT)
        turn_ps = bank[3]
        comb_turn_ps = bank[6]
        b2_ps = bank[7][:].rearrange("p (t f) -> p t f", t=GT)
        wrow_ps = bank[6]
        logit_ps = bank[4][:, 0:GT * E].rearrange("p (t e) -> p t e", t=GT)
        deg_ps = bank[4][:, GT * E:GT * E + GT]
        rank_ps = bank[5][:, 0:GT * E].rearrange("p (t e) -> p t e", t=GT)
        xt_ps = [bank[6], bank[7]]
        up_ps = [bank[0], bank[1]]
        down_ps = [bank[2], bank[3], bank[4], bank[5]]
        last_ps = bank[2]

        adj_sb = sb("adj_ring", [P, RING, CJ, GN])
        z_hi = sb("z_hi", [P, SPLIT * CJ, D], F32R)
        z_lo = sb("z_lo", [P, SPLIT * CJ, D], F32R)
        high = sb("adj_high", [P, PARTS, CJ, GN], F32R)
        low = sb("adj_low", [P, PARTS, CJ, GN], F32R)
        x_sb = sb("x_sb", [P, TILES, D])
        z_sb = sb("z_sb", [P, TILES, D])
        gnn_w_sb = sb("gnn_w_sb", [P, D])
        gnn_wd = sb("gnn_w_less_last_row", [P, D])
        gnn_b_sb = sb("gnn_b_sb", [P, D])
        wr_sb = sb("wr_sb", [P, E])
        br_sb = sb("br_sb", [P, E])
        b2_sb = sb("b2_sb", [E, D])
        beta_sb = sb("beta_sb", [P, TILES])
        ident = sb("ident", [P, P])
        last_row = sb("last_row", [P, P])
        before = sb("before", [P, P], BF16)
        ones_b = sb("ones_b", [P, P], BF16)
        ones_f = sb("ones_f", [P, P])
        iota_e = sb("iota_e", [P, E])
        iota_back = sb("iota_back", [P, 1])
        iota_part = sb("iota_part", [P, 1])
        answer_tab = sb("answer_tab", [P, TILES, K])
        eps_sb = sb("eps_sb", [P, 1])
        pad_row = sb("pad_row", [P, ROW])
        stats = sb("stats", [P, NT, 6])
        mv = sb("mv", [P, NT, 2])
        std = sb("std", [P, NT])
        rstd = sb("rstd", [P, NT])
        zi = sb("zi", [P, GT, D])
        diag = sb("diag", [P, GT, P])
        agg_sb = sb("agg_sb", [P, GN])
        scale = sb("scale", [P, GT])
        agg_out = sb("agg_out", [P, GT, D])
        payload = sb("payload", [P, 2, GT, K, ROW])
        z1t = sb("z1t", [P, GN])
        logits = sb("logits", [P, GT, E])
        top = sb("top", [P, GT, 8])
        top_i = sb("top_i", [P, GT, 8], U32)
        chosen = sb("chosen", [P, GT, K])
        hot = sb("hot", [P, GT, K, E])
        mask = sb("mask", [P, GT, E], BF16)
        seen = sb("seen", [P, E], BF16)
        more = sb("more", [P, E])
        diff = sb("diff", [P, GT])
        ex = sb("ex", [P, GT])
        den = sb("den", [P, GT])
        gates = sb("gates", [P, TILES, K])
        work = sb("work", [P, GT, K, E])
        rank = sb("rank", [P, GT * K])
        slot = sb("slot", [P, 2, GT * K], I32)
        comb = sb("comb", [P, GT, E])
        combt = sb("combt", [E, GN])
        spare = sb("spare", [P, E])
        cnt_i = sb("cnt_i", [P, E], I32)
        tiles_i = sb("tiles_i", [P, E], I32)
        tiles_f = sb("tiles_f", [P, E])
        upto = sb("upto", [P, E])
        past = sb("past", [P, E])
        lw = sb("lw", [P, E])
        own_spare = sb("own_spare", [P, E])
        in_use, expert, first, latest, wanted, taken_row, start_row, again = (
            sb(name, [P, 1])[:] for name in ("in_use", "expert", "first", "latest", "wanted", "taken_row", "start_row", "again"))
        lst = sb("lst", [P, 2])
        q_i = sb("q_i", [P, 2], I32)
        again_diag = sb("again_diag", [P, P])
        skip_tab = sb("skip_tab", [P, P + 1])
        table = sb("table", [2, P], I32)
        ring = adj_sb[:].rearrange("p k u n -> p (k u n)")
        taken = 0

        def in_ring(cols, pattern, **sizes):
            nonlocal taken
            taken += cols
            assert taken <= RING * CJ * GN
            return ring[:, taken - cols:taken].rearrange(pattern, **sizes)

        w_sb = in_ring(SLOTS * WCOLS, "p (s c) -> p s c", s=SLOTS)
        xin = in_ring(SLOTS * ROW, "p (s c) -> p s c", s=SLOTS)
        xt_sb = sb("xt_sb", [P, 2, P])
        h_sb = in_ring(DEEP * HC * P, "p (b c t) -> p b c t", b=DEEP, c=HC)
        y_sb = in_ring(SLOTS * D, "p (s f) -> p s f", s=SLOTS)
        ans = sb("ans", [P, SLOTS], I32)
        taken = 0
        y_in = in_ring(TILES * K * D, "p (t k f) -> p t k f", t=TILES, k=K)

        x_first = sem("x_first")
        x_in = sem("x_in")
        params_in = sem("params_in")
        adj_in = [sem(f"adj_in{k}") for k in range(RING)]
        prefilled = sem("prefilled")
        consts = sem("consts")
        ones_ready = sem("ones_ready")
        passed = sem("passed")
        pool_own = sem("pool_own")
        dve_own = sem("dve_own")
        var0 = sem("var0")
        std0 = sem("std0")
        z_ready = sem("z_ready")
        z_hi_ready = sem("z_hi_ready")
        z_lo_ready = sem("z_lo_ready")
        hi_ready = sem("hi_ready")
        lo_ready = sem("lo_ready")
        bias_added = sem("bias_added")
        wrow_done = sem("wrow_done")
        wd_ready = sem("wd_ready")
        chunk_used = sem("chunk_used")
        own_ready = sem("own_ready")
        agg_done = sem("agg_done")
        agg_copied = sem("agg_copied")
        gnn_done = sem("gnn_done")
        var1 = sem("var1")
        std1 = sem("std1")
        z1_ready = sem("z1_ready")
        z1_turned = sem("z1_turned")
        z1t_ready = sem("z1t_ready")
        logits_done = sem("logits_done")
        mask_ready = sem("mask_ready")
        seen_ready = sem("seen_ready")
        rank_done = sem("rank_done")
        diff_ready = sem("diff_ready")
        ex_ready = sem("ex_ready")
        slots_ready = sem("slots_ready")
        payload_free = sem("payload_free")
        scattered = sem("scattered")
        comb_ready = sem("comb_ready")
        comb_turned = sem("comb_turned")
        combt_ready = sem("combt_ready")
        b2_done = sem("b2_done")
        base_ready = sem("base_ready")
        total_done = sem("total_done")
        list_ready = sem("list_ready")
        list_turned = sem("list_turned")
        table_ready = sem("table_ready")
        tile_in = [sem(f"tile_in{s}") for s in range(SLOTS)]
        x_turned = sem("x_turned")
        xt_ready = sem("xt_ready")
        up_done = sem("up_done")
        h_ready = sem("h_ready")
        down_done = sem("down_done")
        y_ready = sem("y_ready")
        y_out = [sem(f"y_out{s}") for s in range(SLOTS)]
        y_back = [sem(f"y_back{c}") for c in range(OUT_STEPS)]
        gates_done = sem("gates_done")
        scaled = sem("scaled")
        o_ready = sem("o_ready")
        stored = sem("stored")


        def quads_in_use(eng):
            return eng.value_load(table[1:2, 0:1], min_val=TILE_CAP // 2 // QUAD, max_val=TILE_CAP // QUAD)

        def load_starts(engine, first, tiles):
            return nc.values_load_multi_w_load_instructions(
                table[0:1, bass.ds(first, tiles)], engines=[engine], min_val=0, max_val=E * EXPERT_ROWS - P)[1]

        def load_weights(eng, start, s):
            eng.dma_start(w_sb[:, s], w_pack[bass.ds(start // EXPERT_ROWS, 1)].rearrange("a p c -> (a p) c")).then_inc(tile_in[s], 16)

        def load_rows(eng, start, s):
            eng.dma_start(xin[:, s], rows[bass.ds(start, P), :]).then_inc(tile_in[s], 16)

        def load_tile(eng, start, s):
            load_weights(eng, start, s)
            load_rows(eng, start, s)

        def ahead(eng, turn, half, quads, steps):
            start, end = half * QUAD, half * QUAD + QUAD
            alike = end - max(distance for distance, _ in steps)

            def run(tiles, with_next):
                for s in tiles:
                    for distance, step in steps:
                        n = s + distance
                        if n < end or with_next:
                            if n < SLOTS:
                                step(turn, n)
                            else:
                                step(turn + 1, n - SLOTS)

            run(range(start, alike), False)
            if quads is None:
                run(range(alike, end), True)
            else:
                with eng.If(turn * 2 + (half + 1) < quads):
                    run(range(alike, end), True)
                with eng.If(turn * 2 + (half + 1) >= quads):
                    run(range(alike, end), False)

        SP, ACTIVATION = mybir.EngineType.SP, mybir.EngineType.Activation

        def nth_split(g, k):
            return g * SPLIT + (k + 1 - SPLIT)

        def arrival(k):
            return k % ARRIVE if k < SPLIT else ARRIVE + k - SPLIT

        def wait_chunk(eng, g, k):
            if k < SPLIT:
                eng.wait_ge(adj_in[arrival(k)], g * (SPLIT // ARRIVE * 16) + (k // ARRIVE * 16 + 16))
            else:
                eng.wait_ge(adj_in[arrival(k)], g * 16 + 16)

        block = ctx.enter_context(nc.Block())

        @block.sync
        def _(sp):
            x_tiles = x.rearrange("(t p) f -> p t f", p=P)
            sp.dma_start(x_sb[:, 0:GT], x_tiles[:, 0:GT]).then_inc(x_first, 16)

            def load_chunk(g, k):
                sp.dma_start(adj_sb[:, arrival(k)], adj_t[g, k] if isinstance(g, int) else adj_t[bass.ds(g, 1), k].rearrange("a p u n -> (a p) u n")).then_inc(adj_in[arrival(k)], 16)

            def next_chunk(g, k):
                if k >= SPLIT:
                    before_g, before_k = g - 1, k
                elif k >= ARRIVE:
                    before_g, before_k = g, k - ARRIVE
                else:
                    before_g, before_k = g - 1, k + SPLIT - ARRIVE
                if before_k < SPLIT and not (isinstance(before_g, int) and before_g == 0):
                    sp.wait_ge(lo_ready, nth_split(before_g, before_k))
                else:
                    sp.wait_ge(chunk_used, before_g * CHUNKS + (before_k + 1))
                load_chunk(g, k)

            for k in range(CHUNKS):
                if k < ARRIVE or k >= SPLIT:
                    load_chunk(0, k)
                else:
                    next_chunk(0, k)
                if k == 0:
                    sp.dma_start(x_sb[:, GT:TILES], x_tiles[:, GT:TILES]).then_inc(x_in, 16)
                if k == 1:
                    sp.dma_start(gnn_w_sb[:], gnn_w).then_inc(params_in, 16)
                    sp.dma_start(beta_sb[:], beta).then_inc(params_in, 16)
                    sp.dma_start(gnn_b_sb[:], gnn_b.partition_broadcast(P)).then_inc(params_in, 16)
                    sp.dma_start(wr_sb[:], wr).then_inc(params_in, 16)
                    sp.dma_start(br_sb[:], br.partition_broadcast(P)).then_inc(params_in, 16)
                    sp.dma_start(b2_sb[:], b2).then_inc(params_in, 16)
            sp.wait_ge(consts, 1)
            first_rows = rows.rearrange("(e s) c -> s e c", e=E)[0:P]
            padded = 0
            for g, pads in enumerate(PADS, 1):
                for k in range(CHUNKS):
                    next_chunk(g, k)
                    for _ in range(pads[k]):
                        sp.dma_start(first_rows[:, padded:padded + EC],
                                     pad_row[:, None, :].to_broadcast([P, EC, ROW])).then_inc(prefilled, 16)
                        padded += EC
            assert padded == E
            with sp.Fori(1 + len(PADS), GROUPS) as g:
                for k in range(CHUNKS):
                    next_chunk(g, k)

            def next_tile(start, turn, s):
                sp.wait_ge(down_done, turn * SLOTS + (s + 1 + DEEP))
                load_tile(sp, start, s)

            sp.wait_ge(table_ready, 1)
            starts = load_starts(SP, 0, SP_SLOTS)
            for s in range(SP_SLOTS):
                load_weights(sp, starts[s], s)
            sp.wait_ge(scattered, 16 * TILES * K)
            for s in range(SP_SLOTS):
                load_rows(sp, starts[s], s)
            quads = quads_in_use(sp)
            with sp.Fori(0, OCTETS - 1) as turn:
                with sp.If(turn * 2 + 2 < quads):
                    starts = load_starts(SP, turn * SLOTS + SLOTS, SP_SLOTS)
                    for s in range(QUAD):
                        next_tile(starts[s], turn, s)
                    with sp.If(turn * 2 + 3 < quads):
                        for s in range(QUAD, SP_SLOTS):
                            next_tile(starts[s], turn, s)
            for s in range(SLOTS):
                sp.wait_ge(y_out[s], ((quads + (1 if s < QUAD else 0)) // 2) * 16)
            answers = y_tok.rearrange("(t p k) f -> p t k f", p=P, k=K)
            for c in range(OUT_STEPS):
                sp.dma_start(y_in[:, c * OUT_CH:(c + 1) * OUT_CH], answers[:, c * OUT_CH:(c + 1) * OUT_CH]).then_inc(y_back[c], 16)
            for c in range(OUT_STEPS):
                sp.wait_ge(o_ready, c + 1)
                sp.dma_start(out.rearrange("(t p) f -> p t f", p=P)[:, c * OUT_CH:(c + 1) * OUT_CH],
                             x_sb[:, c * OUT_CH:(c + 1) * OUT_CH]).then_inc(stored, 16)
            sp.wait_ge(stored, 16 * OUT_STEPS)

        @block.gpsimd
        def _(pool):
            own = Steps(pool, pool_own)
            pool.memset(ones_b[:], 1.0).then_inc(ones_ready, 1)
            pool.memset(pad_row[:], 0.0)
            pool.memset(ident[:], 0.0)
            pool.memset(last_row[:], 0.0)
            pool.memset(before[:], 0.0)
            pool.memset(ones_f[:], 1.0)
            pool.memset(seen[:], 0.0)
            pool.memset(eps_sb[:], EPS)
            own.after(pool.memset(payload[:], 0.0))
            pool.memset(pad_row[:, ANSWER:ANSWER + 1], float(NO_ANSWER))
            pool.affine_select(out=ident[:], in_=ident[:], compare_op=ALU.not_equal, fill=1.0, base=0,
                               pattern=[[-1, P]], channel_multiplier=1)
            pool.affine_select(out=last_row[:], in_=last_row[:], compare_op=ALU.not_equal, fill=1.0, base=1 - P,
                               pattern=[[0, P]], channel_multiplier=1)
            pool.affine_select(out=before[:], in_=before[:], compare_op=ALU.is_ge, fill=1.0, base=0,
                               pattern=[[-1, P]], channel_multiplier=1)
            pool.iota(iota_e[:], [[1, E]], base=0, channel_multiplier=0, allow_small_or_imprecise_dtypes=True)
            pool.iota(iota_back[:], [[0, 1]], base=-P, channel_multiplier=1, allow_small_or_imprecise_dtypes=True)
            pool.iota(iota_part[:], [[0, 1]], base=0, channel_multiplier=1, allow_small_or_imprecise_dtypes=True)
            pool.iota(answer_tab[:], [[P * K, TILES], [1, K]], base=0, channel_multiplier=K,
                      allow_small_or_imprecise_dtypes=True)
            own.after(pool.memset(z_sb[:, :, D - 1:D], 1.0))
            pool.sem_inc(consts, 1)
            pool.sem_inc(payload_free, 2)
            pool.wait_ge(params_in, 16 * 6)
            def add_bias(c):
                lone_wait(pool, z_ready, c * GT + GT, passed)
                xs = x_sb[:, bass.ds(c * GT, GT), :]
                pool.tensor_tensor(xs, xs, gnn_b_sb[:, None, :].to_broadcast([P, GT, D]), ALU.add).then_inc(bias_added, 1)

            with pool.Fori(0, SPLIT * CJ // GT) as c:
                add_bias(c)
                lone_wait(pool, z_hi_ready, c * GT + GT, passed)
                tiles = bass.ds(c * GT, GT)
                pool.tensor_tensor(z_lo[:, tiles, :], z_sb[:, tiles, :], z_hi[:, tiles, :].bitcast(F32), ALU.subtract).then_inc(z_lo_ready, 1)
            with pool.Fori(SPLIT * CJ // GT, GROUPS) as c:
                add_bias(c)

            def own_rows(tiles):
                pool.tensor_copy(zi[:], z_sb[:, tiles, :])
                pool.tensor_tensor(diag[:], ident[:, None, :].to_broadcast([P, GT, P]),
                                   beta_sb[:, tiles].to_broadcast([P, GT, P]), ALU.mult).then_inc(own_ready, 1)

            def dispatch(g, b):
                lone_wait(pool, z1_ready, g + 1, passed)
                pool.tensor_copy(payload[:, b, :, 1, 0:D], payload[:, b, :, 0, 0:D]).then_inc(pool_own, 1)
                pool.tensor_copy(payload[:, b, :, :, ANSWER], answer_tab[:, bass.ds(g * GT, GT), :]).then_inc(pool_own, 1)
                lone_wait(pool, pool_own, g * 2 + (own.n + 2), passed)
                pool.wait_ge(prefilled, 16 * (E // EC))
                lone_wait(pool, slots_ready, g + 1, passed)
                for t in range(GT):
                    for k in range(K):
                        i = t * K + k
                        pool.indirect_dma_start(rows, bass.IndirectOffsetOnAxis(ap=slot[:, b, i:i + 1], axis=0),
                                                payload[:, b, t, k, :], None).then_inc(scattered, 16)
                pool.wait_ge(scattered, g * (GT * K * 16) + GT * K * 16)
                pool.sem_inc(payload_free, 1)

            own_rows(slice(0, GT))

            def next_own_rows(g):
                lone_wait(pool, agg_done, g + 2, passed)
                own_rows(bass.ds(g * GT + GT, GT))

            next_own_rows(0)
            with pool.Fori(0, GROUPS // 2 - 1) as i:
                for b in range(2):
                    next_own_rows(i * 2 + (b + 1))
                    dispatch(i * 2 + b, b)
            dispatch(GROUPS - 2, 0)
            dispatch(GROUPS - 1, 1)

            pool.wait_ge(table_ready, 1)
            quads = quads_in_use(pool)
            with pool.Fori(0, OCTETS) as turn:
                for half in range(2):
                    with pool.If(turn * 2 + half < quads):
                        for s in range(half * QUAD, half * QUAD + QUAD):
                            lone_wait(pool, y_ready, turn * SLOTS + (s + 1 + DEEP), passed)
                            pool.indirect_dma_start(y_tok, bass.IndirectOffsetOnAxis(ap=ans[:, s:s + 1], axis=0),
                                                    y_sb[:, s, :], None, bounds_check=N * K - 1,
                                                    oob_is_err=False).then_inc(y_out[s], 16)

        @block.scalar
        def _(act):
            act.wait_ge(consts, 1)
            def root_z(step, count):
                act.wait_ge(var0, step + 1)
                nc.scalar.activation(std[:, 0:count], mv[:, 0:count, 1], ACT.Sqrt, bias=eps_sb[:]).then_inc(std0, 1)

            def high_z(first, count):
                act.wait_ge(z_ready, first + count)
                nc.scalar.copy(z_hi[:, bass.ds(first, count), :], z_sb[:, bass.ds(first, count), :]).then_inc(z_hi_ready, count)

            root_z(0, GT)
            root_z(1, GT)
            high_z(0, NT)
            with act.Fori(1, SPLIT * CJ // NT) as i:
                root_z(i + 1, NT)
                high_z(i * NT, NT)
            root_z(TILES // NT, NT)

            def round_chunk(g, k):
                wait_chunk(act, g, k)
                if k >= PARTS:
                    act.wait_ge(chunk_used, g * CHUNKS + (k - PARTS + 1))
                elif not isinstance(g, int) or g > 1:
                    act.wait_ge(chunk_used, g * CHUNKS + (k + SPLIT - PARTS + 1 - CHUNKS))
                nc.scalar.copy(high[:, k % PARTS], adj_sb[:, arrival(k)]).then_inc(hi_ready, 1)

            def copy_agg(p, b):
                act.wait_ge(agg_done, p + 2)
                nc.scalar.copy(agg_sb[:], agg_ps[b][:]).then_inc(agg_copied, 1)

            def root(p):
                act.wait_ge(var1, p + 1)
                nc.scalar.activation(std[:, 0:GT], mv[:, 0:GT, 1], ACT.Sqrt, bias=eps_sb[:]).then_inc(std1, 1)

            def copy_z1t(p):
                act.wait_ge(z1_turned, p + 1)
                nc.scalar.copy(z1t[:], turn_ps[:]).then_inc(z1t_ready, 1)

            def gate_exp(p):
                act.wait_ge(diff_ready, p + 1)
                nc.scalar.activation(ex[:], diff[:], ACT.Exp).then_inc(ex_ready, 1)

            def copy_combt(q):
                act.wait_ge(comb_turned, q + 1)
                nc.scalar.copy(combt[:], comb_turn_ps[0:E, :]).then_inc(combt_ready, 1)

            def alongside(g, b, comb_too, more):
                copy_agg(g - 1, 1 - b)
                if not comb_too:
                    round_chunk(g, 2)
                round_chunk(g, 3)
                if comb_too:
                    copy_combt(g - 2)
                root(g - 1)
                round_chunk(g, 4)
                round_chunk(g, 5)
                copy_z1t(g - 1)
                with more():
                    round_chunk(g + 1, 0)
                gate_exp(g - 1)
                with more():
                    round_chunk(g + 1, 1)
                    round_chunk(g + 1, 2)

            round_chunk(1, 0)
            round_chunk(1, 1)
            alongside(1, 1, False, nullcontext)
            with act.Fori(1, GROUPS // 2) as i:
                alongside(i * 2, 0, True, nullcontext)
                alongside(i * 2 + 1, 1, True, lambda: act.If(i < GROUPS // 2 - 1))
            copy_agg(GROUPS - 1, 1)
            copy_combt(GROUPS - 2)
            root(GROUPS - 1)
            copy_z1t(GROUPS - 1)
            gate_exp(GROUPS - 1)
            copy_combt(GROUPS - 1)
            act.sem_inc(y_ready, DEEP)
            act.wait_ge(table_ready, 1)

            def copy_y(turn, s):
                act.wait_ge(down_done, turn * SLOTS + (s + 1 + DEEP))
                nc.scalar.copy(y_sb[:, s, :], down_ps[s % DEEP][:, 0:D]).then_inc(y_ready, 1)

            starts = load_starts(ACTIVATION, SP_SLOTS, SLOTS - SP_SLOTS)
            act.wait_ge(scattered, 16 * TILES * K)
            for s in range(SP_SLOTS, SLOTS):
                load_tile(act, starts[s - SP_SLOTS], s)
            quads = quads_in_use(act)

            def copy_octet(turn):
                for half in range(2):
                    with act.If(turn * 2 + half < quads):
                        for s in range(half * QUAD, half * QUAD + QUAD):
                            copy_y(turn, s)

            with act.Fori(0, OCTETS - 1) as turn:
                with act.If(turn * 2 + 3 < quads):
                    starts = load_starts(ACTIVATION, turn * SLOTS + (SLOTS + SP_SLOTS), SLOTS - SP_SLOTS)
                    for s in range(SLOTS):
                        copy_y(turn, s)
                        if s >= SP_SLOTS:
                            load_tile(act, starts[s - SP_SLOTS], s)
                with act.If(turn * 2 + 3 >= quads):
                    copy_octet(turn)
            copy_octet(OCTETS - 1)

            act.wait_ge(gates_done, 1)
            for c in range(OUT_STEPS):
                act.wait_ge(y_back[c], 16)
                for t in range(c * OUT_CH, (c + 1) * OUT_CH):
                    last = nc.scalar.activation(y_in[:, t, 1, :], y_in[:, t, 1, :], ACT.Identity, scale=gates[:, t, 1:2])
                last.then_inc(scaled, 1)

        @block.vector
        def _(dve):
            own = Steps(dve, dve_own)
            v = nc.vector
            dve.wait_ge(consts, 1)
            dve.wait_ge(x_first, 16)
            def norm_x(step, first, count):
                for t in range(count):
                    last = v.bn_stats(stats[:, t, :], x_sb[:, bass.ds(first + t, 1), :].rearrange("p a f -> p (a f)"))
                own.after(last, passed)
                for t in range(count):
                    last = v.bn_aggr(mv[:, t, :], stats[:, t, :])
                last.then_inc(var0, 1)
                dve.wait_ge(std0, step + 1)
                own.after(v.reciprocal(rstd[:, 0:count], std[:, 0:count]))
                for t in range(count):
                    xs = x_sb[:, bass.ds(first + t, 1), 0:D - 1].rearrange("p a f -> p (a f)")
                    zs = z_sb[:, bass.ds(first + t, 1), 0:D - 1].rearrange("p a f -> p (a f)")
                    v.tensor_scalar(zs, xs, mv[:, t, 0:1], rstd[:, t:t + 1], ALU.subtract, ALU.mult).then_inc(z_ready, 1)
                dve.wait_ge(z_ready, first + count)

            norm_x(0, 0, GT)
            dve.wait_ge(x_in, 16)
            norm_x(1, GT, GT)
            with dve.Fori(1, TILES // NT) as i:
                own.enter(i - 1, 2)
                norm_x(i + 1, i * NT, NT)
                own.leave(TILES // NT - 1)

            def low_part(g, k):
                dve.wait_ge(hi_ready, nth_split(g, k))
                v.tensor_tensor(low[:, k % PARTS], adj_sb[:, arrival(k)], high[:, k % PARTS].bitcast(F32),
                                ALU.subtract).then_inc(lo_ready, 1)

            def residual(p):
                dve.wait_ge(bias_added, p + 1)
                dve.wait_ge(gnn_done, p + 1)
                xs = x_sb[:, bass.ds(p * GT, GT), :]
                own.after(v.reciprocal(scale[:], deg_ps))
                own.after(v.tensor_tensor(agg_out[:], gnn_ps, scale[:].to_broadcast([P, GT, D]), ALU.mult))
                own.after(v.tensor_tensor(xs, agg_out[:], xs, ALU.add), passed)
                for t in range(GT):
                    last = v.bn_stats(stats[:, t, :], x_sb[:, bass.ds(p * GT + t, 1), :].rearrange("p a f -> p (a f)"))
                own.after(last, passed)
                for t in range(GT):
                    last = v.bn_aggr(mv[:, t, :], stats[:, t, :])
                last.then_inc(var1, 1)

            def normalise(p, b):
                dve.wait_ge(std1, p + 1)
                own.after(v.reciprocal(rstd[:, 0:GT], std[:, 0:GT]))
                dve.wait_ge(payload_free, p + 1)
                for t in range(GT):
                    xs = x_sb[:, bass.ds(p * GT + t, 1), :].rearrange("p a f -> p (a f)")
                    last = v.tensor_scalar(payload[:, b, t, 0, 0:D], xs, mv[:, t, 0:1], rstd[:, t:t + 1],
                                           ALU.subtract, ALU.mult)
                last.then_inc(z1_ready, 1)

            def choose(p):
                dve.wait_ge(logits_done, p + 1)
                own.after(v.tensor_tensor(logits[:], logit_ps, br_sb[:, None, :].to_broadcast([P, GT, E]), ALU.add), passed)
                for t in range(GT):
                    last = v.max(top[:, t, :], logits[:, t, :])
                own.after(last, passed)
                for t in range(GT):
                    last = v.max_index(top_i[:, t, :], top[:, t, :], logits[:, t, :])
                own.after(last)
                v.tensor_tensor(diff[:], top[:, :, 1], top[:, :, 0], ALU.subtract).then_inc(diff_ready, 1)
                own.after(v.tensor_copy(chosen[:], top_i[:, :, 0:K]))
                own.after(v.tensor_tensor(hot[:].rearrange("p t k e -> p (t k) e"),
                                          iota_e[:, None, :].to_broadcast([P, GT * K, E]),
                                          chosen[:].rearrange("p t k -> p (t k)").to_broadcast([P, GT * K, E]), ALU.is_equal))
                v.tensor_tensor(mask[:], hot[:, :, 0, :], hot[:, :, 1, :], ALU.add).then_inc(mask_ready, 1)

            def place(p, b):
                dve.wait_ge(mask_ready, p + 1)
                own.after(v.tensor_reduce(more[:], mask[:].rearrange("p t e -> p e t"), AX_X, ALU.add))
                dve.wait_ge(rank_done, p + 1)
                v.tensor_tensor(seen[:], seen[:], more[:], ALU.add).then_inc(seen_ready, 1)
                for k in range(K):
                    last = v.tensor_tensor(work[:, :, k, :], hot[:, :, k, :], rank_ps, ALU.mult)
                own.after(last)
                own.after(v.tensor_reduce(rank[:], work[:].rearrange("p t k e -> p (t k) e"), AX_X, ALU.add))
                v.scalar_tensor_tensor(out=slot[:, b], in0=chosen[:].rearrange("p t k -> p (t k)"), scalar=float(EXPERT_ROWS),
                                       in1=rank[:], op0=ALU.mult, op1=ALU.add).then_inc(slots_ready, 1)

            def gate(p):
                dve.wait_ge(ex_ready, p + 1)
                own.after(v.tensor_scalar(den[:], ex[:], 1.0, None, ALU.add))
                gs = gates[:, bass.ds(p * GT, GT), :]
                own.after(v.reciprocal(den[:], den[:]))
                v.tensor_copy(gs[:, :, 0], den[:])
                own.after(v.tensor_tensor(gs[:, :, 1], ex[:], den[:], ALU.mult))
                own.after(v.tensor_tensor(work[:].rearrange("p t k e -> p (t k) e"), hot[:].rearrange("p t k e -> p (t k) e"),
                                          gs.rearrange("p t k -> p (t k)").to_broadcast([P, GT * K, E]), ALU.mult))
                v.tensor_tensor(comb[:], work[:, :, 0, :], work[:, :, 1, :], ALU.add).then_inc(comb_ready, 1)

            def base(q):
                dve.wait_ge(b2_done, q + 1)
                xs = x_sb[:, bass.ds(q * GT, GT), :]
                v.tensor_tensor(xs, xs, b2_ps, ALU.add).then_inc(base_ready, 1)

            def alongside(g, b, base_too, more):
                residual(g - 1)
                low_part(g, 3)
                normalise(g - 1, 1 - b)
                if base_too:
                    base(g - 2)
                low_part(g, 4)
                low_part(g, 5)
                choose(g - 1)
                with more():
                    low_part(g + 1, 0)
                place(g - 1, 1 - b)
                with more():
                    low_part(g + 1, 1)
                gate(g - 1)
                with more():
                    low_part(g + 1, 2)

            dve.wait_ge(wrow_done, 1)
            v.tensor_tensor(gnn_wd[:], gnn_w_sb[:], wrow_ps[:, 0:D], ALU.subtract).then_inc(wd_ready, 1)
            for k in range(PARTS):
                low_part(1, k)
            alongside(1, 1, False, nullcontext)
            with dve.Fori(1, GROUPS // 2) as i:
                own.enter(i - 1, 2 * 17)
                alongside(i * 2, 0, True, nullcontext)
                alongside(i * 2 + 1, 1, True, lambda: dve.If(i < GROUPS // 2 - 1))
                own.leave(GROUPS // 2 - 1)
            residual(GROUPS - 1)
            normalise(GROUPS - 1, 1)
            base(GROUPS - 2)
            choose(GROUPS - 1)
            place(GROUPS - 1, 1)

            dve.wait_ge(total_done, 1)
            v.tensor_scalar(spare[:], last_ps[:, 0:E], float(-P), 0.0, ALU.add, ALU.max)
            own.after(v.tensor_scalar(cnt_i[:], last_ps[:, 0:E], float(P - 1), None, ALU.add))
            own.after(v.tensor_scalar(tiles_i[:], cnt_i[:], 7, None, ALU.logical_shift_right))
            own.after(v.tensor_copy(tiles_f[:], tiles_i[:]))
            own.after(v.tensor_tensor_scan(upto[:], tiles_f[:], ones_f[:, 0:E], 0.0, ALU.add, ALU.mult))
            total = upto[:, E - 1:E]
            v.tensor_scalar(past[:], upto[:], iota_part[:], None, ALU.is_le)
            v.scalar_tensor_tensor(out=lw[:], in0=upto[:], scalar=iota_part[:], in1=upto[:], op0=ALU.is_le, op1=ALU.mult)
            v.tensor_tensor(in_use, iota_part[:], total, ALU.is_lt)
            own.after(v.tensor_scalar(q_i[:, 0:1], total, float(QUAD - 1), None, ALU.add))
            v.tensor_scalar(q_i[:, 1:2], q_i[:, 0:1], 2, None, ALU.logical_shift_right)
            own.after(v.tensor_reduce(expert, past[:], AX_X, ALU.add))
            v.tensor_reduce(first, lw[:], AX_X, ALU.max)
            own.after(v.scalar_tensor_tensor(out=own_spare[:], in0=iota_e[:], scalar=expert, in1=spare[:], op0=ALU.is_equal, op1=ALU.mult))
            own.after(v.tensor_reduce(latest, own_spare[:], AX_X, ALU.add))
            own.after(v.tensor_scalar(wanted, iota_part[:], first, float(P), ALU.subtract, ALU.mult))
            own.after(v.tensor_tensor(taken_row, wanted, latest, ALU.min))
            own.after(v.scalar_tensor_tensor(out=start_row, in0=expert, scalar=float(EXPERT_ROWS), in1=taken_row,
                                             op0=ALU.mult, op1=ALU.add))
            v.tensor_tensor(lst[:, 0:1], start_row, in_use, ALU.mult)
            v.tensor_copy(lst[:, 1:2], q_i[:, 1:2])
            own.after(v.tensor_tensor(again, wanted, taken_row, ALU.subtract))
            own.after(v.tensor_scalar(again, again, float(-P), in_use, ALU.add, ALU.mult))
            own.after(v.tensor_scalar(again_diag[:], ident[:], again, None, ALU.mult))
            dve.sem_inc(list_ready, 1)
            dve.wait_ge(list_turned, 1)
            v.tensor_copy(table[:], last_ps[0:2, 0:P]).then_inc(table_ready, 1)
            own.after(v.tensor_scalar(skip_tab[:, 0:P], last_ps[:, P:2 * P], iota_back[:], float(SKIP), ALU.is_gt, ALU.mult))
            gate(GROUPS - 1)
            base(GROUPS - 1)
            dve.sem_inc(gates_done, 1)
            dve.sem_inc(xt_ready, BUFS)
            dve.sem_inc(h_ready, BUFS)

            quads = quads_in_use(dve)

            def copy_xt(turn, s):
                dve.wait_ge(x_turned, turn * SLOTS + (s + 1 + BUFS))
                dve.wait_ge(up_done, turn * SLOTS + (s + 1))
                v.tensor_copy(xt_sb[:, s % 2, :], xt_ps[s % 2][:, 0:P]).then_inc(xt_ready, 1)

            def relu(turn, s):
                if not isinstance(turn, int) or turn > 0:
                    dve.wait_ge(y_out[s], turn * 16)
                v.tensor_tensor(ans[:, s:s + 1], xin[:, s, ANSWER:ANSWER + 1],
                                skip_tab[:, bass.ds(turn * SLOTS + s, 1)], ALU.add)
                dve.wait_ge(up_done, turn * SLOTS + (s + 1 + BUFS))
                dve.wait_ge(down_done, turn * SLOTS + (s + 1))
                for c in range(HC):
                    last = v.tensor_scalar(h_sb[:, s % DEEP, c, :], up_ps[s % 2][:, c * P:(c + 1) * P],
                                           w_sb[:, s, H + HC * D + c:H + HC * D + c + 1], 0.0, ALU.add, ALU.max)
                last.then_inc(h_ready, 1)

            steps = [(1, relu), (3, copy_xt)]
            copy_xt(0, 0)
            copy_xt(0, 1)
            relu(0, 0)
            copy_xt(0, 2)
            for half in range(2):
                ahead(dve, 0, half, None, steps)
            with dve.Fori(1, OCTETS) as turn:
                for half in range(2):
                    with dve.If(turn * 2 + half < quads):
                        ahead(dve, turn, half, quads, steps)

            for c in range(OUT_STEPS):
                tiles = range(c * OUT_CH, (c + 1) * OUT_CH)
                dve.wait_ge(y_back[c], 16)
                for t in tiles:
                    last = v.scalar_tensor_tensor(out=x_sb[:, t, :], in0=y_in[:, t, 0, :], scalar=gates[:, t, 0:1],
                                                  in1=x_sb[:, t, :], op0=ALU.mult, op1=ALU.add)
                own.after(last)
                dve.wait_ge(scaled, c + 1)
                xs = x_sb[:, tiles[0]:tiles[-1] + 1, :]
                v.tensor_tensor(xs, xs, y_in[:, tiles[0]:tiles[-1] + 1, 1, :], ALU.add).then_inc(o_ready, 1)

        @block.tensor
        def _(pe):
            mm = nc.tensor.matmul

            def warm(products, where):
                for _ in range(products):
                    mm(where[:], ones_b[:], ones_b[:, None, :].to_broadcast([P, GT, P]), start=True, stop=True)

            pe.wait_ge(ones_ready, 1)
            warm(14, bank[7])
            pe.wait_ge(consts, 1)
            pe.sem_inc(agg_done, 1)

            def gnn(g):
                if not isinstance(g, int) or g > 0:
                    pe.wait_ge(seen_ready, g)
                pe.wait_ge(wd_ready, 1)
                pe.wait_ge(agg_copied, g + 1)
                for t in range(GT):
                    mm(gnn_ps[:, t, :], agg_sb[:, t * P:(t + 1) * P], gnn_wd[:], start=True, stop=True)
                for t in range(GT):
                    last = mm(deg_ps[:, t:t + 1], agg_sb[:, t * P:(t + 1) * P], last_row[:, 0:1], start=True, stop=True)
                last.then_inc(gnn_done, 1)

            def turn_z1(g, b):
                pe.wait_ge(z1_ready, g + 1)
                for t in range(GT):
                    last = nc.tensor.transpose(turn_ps[:, t * P:(t + 1) * P], payload[:, b, t, 0, 0:D], ident[:])
                last.then_inc(z1_turned, 1)

            def router(g):
                pe.wait_ge(z1t_ready, g + 1)
                for t in range(GT):
                    last = mm(logit_ps[:, t, :], z1t[:, t * P:(t + 1) * P], wr_sb[:], start=True, stop=True)
                last.then_inc(logits_done, 1)

            def ranks(g):
                pe.wait_ge(mask_ready, g + 1)
                mm(rank_ps, before[:], mask[:], start=True, stop=False)
                mm(rank_ps, ones_b[:], seen[:, None, :].to_broadcast([P, GT, E]), start=False, stop=False)
                for t in range(1, GT):
                    last = mm(rank_ps[:, t:GT, :], ones_b[:], mask[:, t - 1:t, :].to_broadcast([P, GT - t, E]),
                              start=False, stop=(t == GT - 1))
                last.then_inc(rank_done, 1)

            def turn_comb(g):
                lone_wait(pe, comb_ready, g + 1, passed)
                for t in range(GT):
                    last = nc.tensor.transpose(comb_turn_ps[0:E, t * P:(t + 1) * P], comb[:, t, :], ident[:])
                last.then_inc(comb_turned, 1)

            def bias2(g):
                pe.wait_ge(combt_ready, g + 1)
                for t in range(GT):
                    last = mm(b2_ps[:, t, :], combt[:, t * P:(t + 1) * P], b2_sb[:], start=True, stop=True)
                last.then_inc(b2_done, 1)

            def own_product(g, b):
                pe.wait_ge(own_ready, g + 1)
                for t in range(GT):
                    last = mm(agg_ps[b][:, t * P:(t + 1) * P], zi[:, t, :], diag[:, t, :], start=False, stop=(t == GT - 1))
                last.then_inc(agg_done, 1)

            def whole_chunk(g, b, k, step):
                wait_chunk(pe, g, k)
                for u in range(CJ):
                    step(k * CJ + u)
                    last = mm(agg_ps[b][:], z_sb[:, k * CJ + u, :], adj_sb[:, arrival(k), u, :], start=(k + u == 0), stop=False)
                last.then_inc(chunk_used, 1)

            def split_chunk(g, b, k, step):
                pe.wait_ge(hi_ready, nth_split(g, k))
                for u in range(CJ):
                    j = k * CJ + u
                    step(j)
                    mm(agg_ps[b][:], z_hi[:, j, :], high[:, k % PARTS, u, :], start=(j == 0), stop=False)
                    mm(agg_ps[b][:], z_lo[:, j, :], high[:, k % PARTS, u, :], start=False, stop=False)
                pe.wait_ge(lo_ready, nth_split(g, k))
                for u in range(CJ):
                    last = mm(agg_ps[b][:], z_hi[:, k * CJ + u, :], low[:, k % PARTS, u, :], start=False, stop=False)
                last.then_inc(chunk_used, 1)

            for k in range(CHUNKS):
                whole_chunk(0, 0, k, lambda j: pe.wait_ge(z_ready, j + 1))
                if k == CHUNKS // 2:
                    pe.wait_ge(params_in, 16 * 6)
                    mm(wrow_ps[:, 0:D], last_row[:], gnn_w_sb[:], start=True, stop=True).then_inc(wrow_done, 1)
            own_product(0, 0)
            pe.wait_ge(z_lo_ready, SPLIT * CJ // GT)

            def aggregate(g, b, gates_too):
                def step(j):
                    if j == 2:
                        gnn(g - 1)
                    if j == 4 and gates_too:
                        turn_comb(g - 2)
                    if j == 8 and gates_too:
                        bias2(g - 2)
                    if j == 14:
                        turn_z1(g - 1, 1 - b)
                    if j == 17:
                        router(g - 1)
                    if j == 25:
                        ranks(g - 1)

                for k in range(CHUNKS):
                    (split_chunk if k < SPLIT else whole_chunk)(g, b, k, step)
                own_product(g, b)

            aggregate(1, 1, False)
            with pe.Fori(1, GROUPS // 2) as i:
                aggregate(i * 2, 0, True)
                aggregate(i * 2 + 1, 1, True)
            gnn(GROUPS - 1)
            turn_comb(GROUPS - 2)
            bias2(GROUPS - 2)
            turn_z1(GROUPS - 1, 1)
            router(GROUPS - 1)
            ranks(GROUPS - 1)
            pe.wait_ge(seen_ready, GROUPS)
            mm(last_ps[:, 0:E], ones_b[:], seen[:], start=True, stop=True).then_inc(total_done, 1)
            warm(13, turn_ps)
            pe.wait_ge(list_ready, 1)
            nc.tensor.transpose(last_ps[0:2, 0:P], lst[:], ident[:])
            mm(last_ps[:, P:2 * P], ones_f[:], again_diag[:], start=True, stop=True).then_inc(list_turned, 1)
            turn_comb(GROUPS - 1)
            bias2(GROUPS - 1)

            warm(6, turn_ps)
            pe.wait_ge(table_ready, 1)
            pe.wait_ge(base_ready, GROUPS)
            pe.sem_inc(x_turned, BUFS)
            pe.sem_inc(up_done, BUFS)
            pe.sem_inc(down_done, DEEP)
            quads = quads_in_use(pe)

            def turn_x(turn, s):
                pe.wait_ge(tile_in[s], turn * 32 + 32)
                pe.wait_ge(xt_ready, turn * SLOTS + (s + 1))
                nc.tensor.transpose(xt_ps[s % 2][:, 0:P], xin[:, s, 0:D], ident[:]).then_inc(x_turned, 1)

            def up(turn, s):
                pe.wait_ge(xt_ready, turn * SLOTS + (s + 1 + BUFS))
                pe.wait_ge(h_ready, turn * SLOTS + (s + 1))
                for c in range(HC):
                    last = mm(up_ps[s % 2][:, c * P:(c + 1) * P], w_sb[:, s, c * P:(c + 1) * P], xt_sb[:, s % 2, :],
                              start=True, stop=True)
                last.then_inc(up_done, 1)

            def down(turn, s):
                pe.wait_ge(h_ready, turn * SLOTS + (s + 1 + BUFS))
                pe.wait_ge(y_ready, turn * SLOTS + (s + 1))
                for c in range(HC):
                    last = mm(down_ps[s % DEEP][:, 0:D], h_sb[:, s % DEEP, c, :], w_sb[:, s, H + c * D:H + (c + 1) * D],
                              start=(c == 0), stop=(c == HC - 1))
                last.then_inc(down_done, 1)

            turn_x(0, 0)
            turn_x(0, 1)
            up(0, 0)
            turn_x(0, 2)
            up(0, 1)
            with pe.Fori(0, OCTETS) as turn:
                for half in range(2):
                    with pe.If(turn * 2 + half < quads):
                        ahead(pe, turn, half, quads, [(3, turn_x), (0, down), (2, up)])


def kernel(x, adj, L0_gnn_kernel, L0_gnn_bias, L0_gnn_beta, L0_ffn_Wr, L0_ffn_br, L0_ffn_W1, L0_ffn_b1, L0_ffn_W2, L0_ffn_b2):
    import concourse.bacc as bacc
    from concourse.bass_utils import run_bass_kernel_spmd

    a = np.asarray
    adj_t = a(adj).reshape(GROUPS, GN, CHUNKS, CJ, P).transpose(0, 2, 4, 3, 1)
    w1 = a(L0_ffn_W1)
    w2 = a(L0_ffn_W2).reshape(E, HC, P, D).transpose(0, 2, 1, 3).reshape(E, P, HC * D)
    b1 = a(L0_ffn_b1).reshape(E, HC, P).transpose(0, 2, 1)
    arrays = {
        "x": a(x), "adj_t": adj_t, "gnn_w": a(L0_gnn_kernel), "gnn_b": a(L0_gnn_bias),
        "beta": a(L0_gnn_beta).reshape(TILES, P).T, "wr": a(L0_ffn_Wr), "br": a(L0_ffn_br),
        "w_pack": np.concatenate([w1, w2, b1], axis=2), "b2": a(L0_ffn_b2),
    }
    arrays = {name: np.ascontiguousarray(v) for name, v in arrays.items()}
    nc = bacc.Bacc("TRN2", target_bir_lowering=False, num_devices=1)
    args = [nc.dram_tensor(name, v.shape, mybir.dt.from_np(v.dtype), kind="ExternalInput").ap() for name, v in arrays.items()]
    out = nc.dram_tensor("out", [N, D], F32, kind="ExternalOutput").ap()
    program(nc, *args, out)
    result = run_bass_kernel_spmd(nc, [arrays], core_ids=[0])
    return result.results[0]["out"]
```
